# Optimizing a Trainium2 kernel written in Bass

```python
import numpy as np
import jax
import jax.numpy as jnp

def _softmax(x, axis=-1):
    return jax.nn.softmax(x, axis=axis)

def _gelu(x):
    return jax.nn.gelu(x, approximate=True)

def _silu(x):
    return jax.nn.silu(x)

def _sigmoid(x):
    return jax.nn.sigmoid(x)

def _layernorm(x, axis=-1, eps=1e-05):
    m = jnp.mean(x, axis=axis, keepdims=True)
    v = jnp.var(x, axis=axis, keepdims=True)
    return (x - m) / jnp.sqrt(v + eps)

def _scatter_add(tgt, idx, src, axis=0):
    return tgt.at[idx].add(src)

def _segment_sum(src, seg, n):
    return jax.ops.segment_sum(src, seg, n)
kernel_name = 'mk_decoder_preln_d1_seqx_r8_1c11e7'

def setup_inputs(seed: int=0):
    np.random.seed(seed)
    _w = jnp.asarray

    def _rec_inputs():
        import jax
        import jax.numpy as jnp
        _rk = jax.random.key(seed)
        x = -0.0003929 + 0.9999 * jax.random.normal(jax.random.fold_in(_rk, 1), (16, 256, 128), jnp.float32)
        _lenS = 256 - jax.random.randint(jax.random.fold_in(_rk, 7), (16,), 0, max(1, 256 // 4) + 1, jnp.int32)
        _lenS2 = 1601 - jax.random.randint(jax.random.fold_in(_rk, 8), (16,), 0, max(1, 1601 // 4) + 1, jnp.int32)
        _ctx_1024P = jax.random.normal(jax.random.fold_in(_rk, 11), (16, 16, 128), jnp.float32)
        _ctx_1024c = jax.random.dirichlet(jax.random.fold_in(_rk, 511), 0.3 * jnp.ones((16,), jnp.float32), (16, 1601))
        _ctx_1024t = jnp.einsum('bsk,bkd->bsd', _ctx_1024c, _ctx_1024P)
        _ctx_1024t = _ctx_1024t * jax.lax.rsqrt(jnp.mean(jnp.square(_ctx_1024t)) + 1e-12) * 0.953939
        ctx_1024 = 2.81802e-05 + 1.00001 * (_ctx_1024t + 0.3 * jax.random.normal(jax.random.fold_in(_rk, 611), (16, 1601, 128), jnp.float32))
        return (x, ctx_1024)
    x, ctx_1024 = _rec_inputs()

    def _L0_attn_setup():
        import jax, jax.numpy as jnp
        import numpy as np
        B, C, D, H = (2, 256, 128, 16)
        HE = D // H
        key = jax.random.key(seed)
        k1, k2, k3, k4, k5 = jax.random.split(key, 5)
        s = 0.02
        return {'x': jax.random.normal(k1, (B, C, D), dtype=jnp.float32), 'Wqkv': jax.random.normal(k2, (HE, 3 * HE), dtype=jnp.float32) * s, 'bqkv': jax.random.normal(k3, (3 * HE,), dtype=jnp.float32) * s, 'Wr': jax.random.normal(k4, (D, D), dtype=jnp.float32) * s, 'br': jax.random.normal(k5, (D,), dtype=jnp.float32) * s}
    _L0_attn_all = _L0_attn_setup()
    _L0_attn_in = {k: v for k, v in _L0_attn_all.items() if k in ('Wqkv', 'bqkv', 'Wr', 'br')}
    del _L0_attn_all

    def _L0_xattn_setup():
        import jax, jax.numpy as jnp
        import numpy as np
        QUERY_DIM = 128
        HIDDEN_DIM = 128
        key = jax.random.key(seed)
        k1, k2, k3, k4 = jax.random.split(key, 4)
        query = jax.random.normal(k1, (8, 256, QUERY_DIM), dtype=jnp.float32)
        info = jax.random.normal(k2, (8, 256, HIDDEN_DIM), dtype=jnp.float32)
        bound = 1.0 / np.sqrt(QUERY_DIM)
        W = jax.random.uniform(k3, (HIDDEN_DIM, QUERY_DIM), jnp.float32, -bound, bound)
        b = jax.random.uniform(k4, (HIDDEN_DIM,), jnp.float32, -bound, bound)
        return {'query': query, 'info': info, 'W': W, 'b': b}
    _L0_xattn_all = _L0_xattn_setup()
    _L0_xattn_in = {k: v for k, v in _L0_xattn_all.items() if k in ('W', 'b')}
    del _L0_xattn_all

    def _L0_ffn_setup():
        import jax, jax.numpy as jnp
        import numpy as np
        DIM = 128
        INTER = 256
        E = 8
        TOPK = 2
        ROUTE_SCALE = 1.0

        def _mlp(x, w1, w2, w3):
            h = jax.nn.silu(x @ w1.T) * (x @ w3.T)
            return h @ w2.T
        key = jax.random.key(seed)
        ks = jax.random.split(key, 10)
        s_in = 0.02
        return {'x': jax.random.normal(ks[0], (4, 256, DIM), dtype=jnp.float32), 'gate_w': jax.random.normal(ks[1], (E, DIM), dtype=jnp.float32) * s_in, 'gate_bias': jax.random.normal(ks[2], (E,), dtype=jnp.float32) * 0.01, 'w1': jax.random.normal(ks[3], (E, INTER, DIM), dtype=jnp.float32) * s_in, 'w2': jax.random.normal(ks[4], (E, DIM, INTER), dtype=jnp.float32) * s_in, 'w3': jax.random.normal(ks[5], (E, INTER, DIM), dtype=jnp.float32) * s_in, 'sw1': jax.random.normal(ks[6], (INTER, DIM), dtype=jnp.float32) * s_in, 'sw2': jax.random.normal(ks[7], (DIM, INTER), dtype=jnp.float32) * s_in, 'sw3': jax.random.normal(ks[8], (INTER, DIM), dtype=jnp.float32) * s_in}
    _L0_ffn_all = _L0_ffn_setup()
    _L0_ffn_in = {k: v for k, v in _L0_ffn_all.items() if k in ('gate_w', 'gate_bias', 'w1', 'w2', 'w3', 'sw1', 'sw2', 'sw3')}
    del _L0_ffn_all
    return {'x': x, 'ctx_1024': ctx_1024, 'L0_attn_Wqkv': _L0_attn_in['Wqkv'], 'L0_attn_bqkv': _L0_attn_in['bqkv'], 'L0_attn_Wr': _L0_attn_in['Wr'], 'L0_attn_br': _L0_attn_in['br'], 'L0_xattn_W': _L0_xattn_in['W'], 'L0_xattn_b': _L0_xattn_in['b'], 'L0_ffn_gate_w': _L0_ffn_in['gate_w'], 'L0_ffn_gate_bias': _L0_ffn_in['gate_bias'], 'L0_ffn_w1': _L0_ffn_in['w1'], 'L0_ffn_w2': _L0_ffn_in['w2'], 'L0_ffn_w3': _L0_ffn_in['w3'], 'L0_ffn_sw1': _L0_ffn_in['sw1'], 'L0_ffn_sw2': _L0_ffn_in['sw2'], 'L0_ffn_sw3': _L0_ffn_in['sw3']}

def reference(x, ctx_1024, L0_attn_Wqkv, L0_attn_bqkv, L0_attn_Wr, L0_attn_br, L0_xattn_W, L0_xattn_b, L0_ffn_gate_w, L0_ffn_gate_bias, L0_ffn_w1, L0_ffn_w2, L0_ffn_w3, L0_ffn_sw1, L0_ffn_sw2, L0_ffn_sw3):
    import jax
    import jax.numpy as jnp

    def _L0_attn_ref(x, Wqkv, bqkv, Wr, br):
        import jax, jax.numpy as jnp
        import numpy as np
        B, C, D, H = (2, 256, 128, 16)
        HE = D // H
        b, c, d = x.shape
        h, he = (H, HE)
        xh = x.reshape(b, c, h, he).transpose(0, 2, 1, 3)
        qkv = jnp.einsum('bhce,ef->bhcf', xh, Wqkv) + bqkv
        q, k, v = jnp.split(qkv, 3, axis=-1)
        att = jnp.einsum('bhqe,bhke->bhqk', q, k) / jnp.sqrt(jnp.float32(he))
        mask = jnp.tril(jnp.ones((c, c), dtype=att.dtype), k=-1)
        att = jax.nn.softmax(att * mask, axis=-1)
        out = jnp.einsum('bhqk,bhke->bhqe', att, v)
        out = out.transpose(0, 2, 1, 3).reshape(b, c, d)
        out = out @ Wr + br
        return out

    def _L0_xattn_ref(query, info, W, b):
        import jax, jax.numpy as jnp
        import numpy as np
        QUERY_DIM = 128
        HIDDEN_DIM = 128
        q = jnp.einsum('bsq,hq->bsh', query, W) + b
        scores = jax.nn.softmax(jnp.einsum('bsh,bmh->bsm', q, info), axis=-1)
        return jnp.einsum('bsm,bmh->bsh', scores, info)

    def _L0_ffn_ref(x, gate_w, gate_bias, w1, w2, w3, sw1, sw2, sw3):
        import jax, jax.numpy as jnp
        import numpy as np
        DIM = 128
        INTER = 256
        E = 8
        TOPK = 2
        ROUTE_SCALE = 1.0

        def _mlp(x, w1, w2, w3):
            h = jax.nn.silu(x @ w1.T) * (x @ w3.T)
            return h @ w2.T
        shape = x.shape
        xt = x.reshape(-1, DIM)
        T = xt.shape[0]
        logits = xt @ gate_w.T
        scores = jax.nn.softmax(logits.astype(jnp.float32), axis=-1)
        original_scores = scores
        biased = scores + gate_bias
        _, indices = jax.lax.top_k(biased, TOPK)
        weights = jnp.take_along_axis(original_scores, indices, axis=1)
        weights = (weights * ROUTE_SCALE).astype(x.dtype)
        combine = (jax.nn.one_hot(indices, E, dtype=weights.dtype) * weights[..., None]).sum(axis=1)
        y = jnp.zeros_like(xt)
        for e in range(E):
            y = y + _mlp(xt, w1[e], w2[e], w3[e]) * combine[:, e:e + 1]
        z = _mlp(xt, sw1, sw2, sw3)
        return (y + z).reshape(shape)
    x = x + _L0_attn_ref(_layernorm(x, axis=-1), L0_attn_Wqkv, L0_attn_bqkv, L0_attn_Wr, L0_attn_br)
    x = x + _L0_xattn_ref(_layernorm(x, axis=-1), ctx_1024, L0_xattn_W, L0_xattn_b)
    x = x + _L0_ffn_ref(_layernorm(x, axis=-1), L0_ffn_gate_w, L0_ffn_gate_bias, L0_ffn_w1, L0_ffn_w2, L0_ffn_w3, L0_ffn_sw1, L0_ffn_sw2, L0_ffn_sw3)
    return x

_drawn_inputs = setup_inputs


def setup_inputs(seed=0):
    import zlib

    import numpy as np

    out = dict(_drawn_inputs(seed))
    spreads = {}
    factors = {'L0_attn_Wqkv': 8.0,
     'L0_attn_bqkv': 7.989,
     'L0_attn_Wr': 8.0,
     'L0_ffn_gate_w': 8.0,
     'L0_ffn_gate_bias': 8.0,
     'L0_ffn_w1': 8.0,
     'L0_ffn_w2': 8.0,
     'L0_ffn_w3': 8.0,
     'L0_ffn_sw1': 8.0,
     'L0_ffn_sw2': 8.0,
     'L0_ffn_sw3': 8.0}
    for name, (base, spread) in spreads.items():
        noise = np.random.default_rng([zlib.crc32(name.encode()), seed]).standard_normal(out[name].shape)
        drawn = base * np.exp(spread * noise) if base else spread * noise
        out[name] = jnp.asarray(drawn.astype(out[name].dtype))
    for name, factor in factors.items():
        out[name] = (out[name] * factor).astype(out[name].dtype)
    return out
```

```python
from contextlib import ExitStack

import numpy as np
import concourse.bass as bass
from concourse import mybir

ALU = mybir.AluOpType
ACT = mybir.ActivationFunctionType
AX = mybir.AxisListType
F32 = mybir.dt.float32
F32R = mybir.dt.float32r
BF16 = mybir.dt.bfloat16
U32 = mybir.dt.uint32

P = 128
B, S, D = 16, 256, 128
T = S // P
NT = B * T
H = 16
HE = D // H
HA = 2
HG = H // HA
NG = 4
M = 1601
MB = M // P
MR = M - MB * P
MF = MB * P
NB = MB + 1
E = 8
INTER = 256
NE = E + 1
EPS = 1e-5
SCALE = float(1.0 / np.sqrt(np.float32(HE)))
NEG = -1.0e30
TERMS_Q = ((0, 3), (0, 2), (0, 1))
QROWS = 48
KROWS = 51

C_ID, C_MASK, C_U, C_ONE, C_CNT, C_BV, C_BR, C_BIAS, C_GB, C_IOTA, C_END = 0, 128, 256, 384, 512, 544, 672, 800, 804, 812, 820


def decoder_kernel(nc, x, ctx, ctxT, consts, wq, wk, wv, wr, wx, gate, w13, w2, out):
    with ExitStack() as stack:
        def sb(name, shape, dt=F32):
            return stack.enter_context(nc.sbuf_tensor(name, shape, dt))

        def sem(name):
            return stack.enter_context(nc.semaphore(name))

        ps = stack.enter_context(nc.psum_tensor("banks", [P, 8, 512], F32))

        dq = nc.dram_tensor("stack_parts", [2, HA, 3, P // HA, S], BF16).ap()
        dm = nc.dram_tensor("max_parts", [3, H, S], BF16).ap()

        cst = sb("cst", [P, C_END])
        ident_bf = sb("ident_bf", [P, P], BF16)
        mask_bf = sb("mask_bf", [P, NG, P], BF16)
        half = sb("half", [P, 2 * T])
        wq_sb, wk_sb, wv_sb = sb("wq_sb", [P, P]), sb("wk_sb", [P, P]), sb("wv_sb", [P, P])
        wr_sb, wx_sb = sb("wr_sb", [P, P]), sb("wx_sb", [P, P])
        gate_sb = sb("gate_sb", [P, E])
        w13_raw = sb("w13_raw", [P, 2 * INTER])
        w13_hi = sb("w13_hi", [P, NE, 2 * INTER], F32R)
        w13_lo = sb("w13_lo", [P, NE, 2 * INTER], F32R)
        w2_sb = sb("w2_sb", [P, NE, INTER // P, D])
        ident = cst[:, C_ID:C_ID + P]
        upper = cst[:, C_U:C_U + P]
        ones = cst[:, C_ONE:C_ONE + P]

        xall = sb("xall", [P, NT, D])

        st = sb("st", [P, T, 6])
        mv = sb("mv", [P, T, 2])
        rstd = sb("rstd", [P, 2, T])
        xn1, xn2 = sb("xn1", [P, T, D]), sb("xn2", [P, T, D])
        xb = sb("xb", [P, T, D])
        xn1T, xn2T = sb("xn1T", [P, S]), sb("xn2T", [P, S])
        st2 = sb("st2", [P, T, 6])
        mv2 = sb("mv2", [P, T, 2])
        rstd2 = sb("rstd2", [P, 2, T])

        qk = sb("qk", [P, 2, S])
        qk_r = sb("qk_r", [P, 2, S])
        parts = sb("parts", [P, 3, 2, S], BF16)
        qst, kst = sb("qst", [P, HG, S], BF16), sb("kst", [P, HG, S], BF16)
        vaug = sb("vaug", [P, T, H, 32])
        mx = sb("mx", [P, T, H])
        negm = sb("negm", [P, T, H])
        em = sb("em", [P, T, H])
        emc = sb("emc", [P, T, H])
        mT = sb("mT", [H, S])
        mT_r = sb("mT_r", [H, S])
        mparts = sb("mparts", [H, 3, S], BF16)
        sv = sb("sv", [P, T, D])
        emsv = sb("emsv", [P, T, D])
        prob = [sb(f"prob{n}", [P, 3 * 512]) for n in range(2)]
        oT = sb("oT", [P, NG, S])
        den = sb("den", [P, T, H])
        rden = sb("rden", [P, T, H])
        num = sb("num", [P, T, D])
        on = sb("on", [P, T, D])
        onT = sb("onT", [P, S])

        q2 = sb("q2", [P, S])
        q2_hi, q2_lo = sb("q2_hi", [P, S], F32R), sb("q2_lo", [P, S], F32R)
        infoT = sb("infoT", [P, M])
        info_hi, info_lo = sb("info_hi", [P, MF], F32R), sb("info_lo", [P, MF], F32R)
        info_tail = sb("info_tail", [P, MR])
        info = sb("info", [P, NB, D])
        xmax = sb("xmax", [P, T])
        xprob = [sb(f"xprob{t}", [P, M]) for t in range(T)]
        xprobT = [sb(f"xprobT{t}", [P, NB, P]) for t in range(T)]
        xsum = sb("xsum", [P, T])
        xrec = sb("xrec", [P, T])

        s = {n: sem(n) for n in (
            "consts_in", "weights_in", "x_first_in", "x_in", "const_done", "w13_in", "w13_raw_done", "w13_step",
            "ln1_stats", "ln1_aggr", "ln1_eps", "ln1_rstd", "xn1_done", "xb_done",
            "xn1T_ps", "xn1T_sb", "qk_ps", "v_ps", "qk_sb", "v_done",
            "split_step", "parts_done", "parts_out", "stack_in",
            "sv_ps", "sv_sb", "alpha_ps", "alpha_max", "max_clip", "negm_done", "mT_ps", "mT_sb",
            "msplit_step", "mparts_out", "mrows_in", "em_done", "emc_done", "emsv_done",
            "gamma_ps", "p_exp", "p_masked", "pv_ps", "oT_sb",
            "o_ps", "den_done", "rden_done", "num_done", "on_done", "onT_ps", "onT_sb", "wr_ps", "x2_done",
            "ln2_stats", "ln2_aggr", "ln2_eps", "ln2_rstd", "xn2_done", "xn2T_ps", "xn2T_sb", "q2_ps", "q2_sb", "q2_hi_done", "q2_lo_done",
            "infoT_in", "info_hi_done", "info_lo_done", "info_in",
            "xs_ps", "xmax_done", "xexp_done", "xt_ps", "xt_act", "xt_dve", "xpv_ps", "xrec_done", "x3_done")}

        def apart(eng, name, value):
            eng.wait_ge(s[name], value)
            eng.sem_inc(passed[eng.engine], 1)

        passed = {e.engine: sem(f"passed_{n}") for n, e in (("dve", nc.vector), ("pool", nc.gpsimd), ("sp", nc.sync))}

        def flat(b0, n):
            return ps[:].rearrange("p b n -> p (b n)")[:, b0 * 512:b0 * 512 + n]

        def heads4(c0):
            return [4 * c0 + c for c in range(4)]

        xn3, xn3T = sb("xn3", [P, D]), sb("xn3T", [P, P])
        x3_hi, x3_lo = sb("x3_hi", [P, P], F32R), sb("x3_lo", [P, P], F32R)
        lmax, esum, erec = sb("lmax", [P, 1]), sb("esum", [P, 1]), sb("erec", [P, 1])
        ex, sc, biased, top = sb("ex", [P, E]), sb("sc", [P, E]), sb("biased", [P, E]), sb("top", [P, 8])
        topi, topf, oh = sb("topi", [P, 8], U32), sb("topf", [P, 2]), sb("oh", [P, E])
        comb = sb("comb", [P, NE])
        hs = [sb(f"hs{n}", [P, INTER]) for n in range(2)]
        h = [sb(f"h{n}", [P, INTER]) for n in range(2)]
        hT = [sb(f"hT{n}", [P, INTER]) for n in range(2)]
        for n in ("ln3_stats", "ln3_aggr", "ln3_eps", "ln3_rstd", "xn3_done", "xn3T_ps", "xn3T_sb", "lg_ps", "lmax_done", "ex_done",
                  "rt", "comb_init", "comb_done", "xT_split", "up_ps", "silu_done", "h_done", "hT_ps", "hT_sb", "y_ps", "y_done"):
            s[n] = sem(n)

        def over_tiles(eng, tile):
            tile(0, False)
            with eng.Fori(1, NT) as k:
                tile(k, True)

        def moe_pe(pe):
            def tile(k, later):
                pe.wait_ge(s["xn3_done"], k + 1)
                if later:
                    pe.wait_ge(s["y_done"], k)
                pe.transpose(ps[:, 0, 0:P], xn3[:], ident).then_inc(s["xn3T_ps"], 1)
                pe.wait_ge(s["xn3T_sb"], k + 1)
                pe.matmul(ps[:, 1, 0:E], lhsT=xn3T[:], rhs=gate_sb[:], start=True, stop=True).then_inc(s["lg_ps"], 1)
                pe.wait_ge(s["xT_split"], 2 * k + 2)

                def up(e):
                    if e >= 2:
                        pe.wait_ge(s["h_done"], NE * k + e - 1)
                        pe.wait_ge(s["silu_done"], NE * k + e - 1)
                    for n, (a, b) in enumerate(((x3_hi, w13_hi), (x3_hi, w13_lo), (x3_lo, w13_hi))):
                        mm = pe.matmul(ps[:, 2 + e % 2, :], lhsT=a[:], rhs=b[:, e, :], start=(n == 0), stop=(n == 2))
                    mm.then_inc(s["up_ps"], 1)

                up(0)
                for e in range(NE):
                    if e + 1 < NE:
                        up(e + 1)
                    pe.wait_ge(s["h_done"], NE * k + e + 1)
                    if e >= 2:
                        pe.wait_ge(s["hT_sb"], NE * k + e - 1)
                    for c in range(2):
                        mm = pe.transpose(ps[:, 4 + e % 2, c * P:(c + 1) * P], h[e % 2][:, c * P:(c + 1) * P], ident)
                    mm.then_inc(s["hT_ps"], 1)
                    pe.wait_ge(s["hT_sb"], NE * k + e + 1)
                    for c in range(2):
                        mm = pe.matmul(ps[:, 6, 0:D], lhsT=hT[e % 2][:, c * P:(c + 1) * P], rhs=w2_sb[:, e, c, :],
                                       start=(e == 0 and c == 0), stop=(e == NE - 1 and c == 1))
                mm.then_inc(s["y_ps"], 1)

            over_tiles(pe, tile)

        def moe_act(act):
            def tile(k, later):
                act.wait_ge(s["xn3T_ps"], k + 1)
                act.copy(xn3T[:], ps[:, 0, 0:P]).then_inc(s["xn3T_sb"], 1)
                act.wait_ge(s["lmax_done"], k + 1)
                act.activation(ex[:], ps[:, 1, 0:E], ACT.Exp, bias=lmax[:], accum_out=esum[:]).then_inc(s["ex_done"], 1)
                for e in range(NE):
                    act.wait_ge(s["up_ps"], NE * k + e + 1)
                    if e >= 2:
                        act.wait_ge(s["h_done"], NE * k + e - 1)
                    act.activation(hs[e % 2][:], ps[:, 2 + e % 2, 0:INTER], ACT.Silu).then_inc(s["silu_done"], 1)
                    act.wait_ge(s["hT_ps"], NE * k + e + 1)
                    act.copy(hT[e % 2][:], ps[:, 4 + e % 2, 0:INTER]).then_inc(s["hT_sb"], 1)

            over_tiles(act, tile)

        def moe_dve(dve):
            dve.memset(comb[:], 1.0).then_inc(s["comb_init"], 1)
            dve.wait_ge(s["comb_init"], 1)
            dve.wait_ge(s["x3_done"], 2 * B)
            def tile(k, later):
                if later:
                    apart(dve, "xn3_done", k)
                dve.bn_stats(st[:, 0, :], xall[:, bass.ds(k, 1), :]).then_inc(s["ln3_stats"], 1)
                apart(dve, "ln3_stats", k + 1)
                dve.bn_aggr(mv[:, 0, :], st[:, 0, :]).then_inc(s["ln3_aggr"], 1)
                dve.wait_ge(s["ln3_rstd"], k + 1)
                dve.tensor_scalar(xn3[:].unsqueeze(1), xall[:, bass.ds(k, 1), :], mv[:, 0, 0:1], rstd[:, 1, 0:1], ALU.subtract, ALU.mult
                                  ).then_inc(s["xn3_done"], 1)
                dve.wait_ge(s["lg_ps"], k + 1)
                dve.tensor_reduce(lmax[:], ps[:, 1, 0:E], AX.X, ALU.max, negate=True).then_inc(s["lmax_done"], 1)
                dve.wait_ge(s["ex_done"], k + 1)
                dve.reciprocal(erec[:], esum[:]).then_inc(s["rt"], 1)
                dve.wait_ge(s["rt"], 8 * k + 1)
                dve.tensor_scalar(sc[:], ex[:], erec[:], None, ALU.mult).then_inc(s["rt"], 1)
                dve.wait_ge(s["rt"], 8 * k + 2)
                dve.tensor_tensor(biased[:], sc[:], cst[:, C_GB:C_GB + E], ALU.add).then_inc(s["rt"], 1)
                apart(dve, "rt", 8 * k + 3)
                dve.max(top[:], biased[:]).then_inc(s["rt"], 1)
                apart(dve, "rt", 8 * k + 4)
                dve.max_index(topi[:], top[:], biased[:]).then_inc(s["rt"], 1)
                dve.wait_ge(s["rt"], 8 * k + 5)
                dve.tensor_copy(topf[:], topi[:, 0:2]).then_inc(s["rt"], 1)
                dve.wait_ge(s["rt"], 8 * k + 6)
                iota = cst[:, C_IOTA:C_IOTA + E]
                dve.tensor_scalar(oh[:], iota, topf[:, 0:1], None, ALU.is_equal).then_inc(s["rt"], 1)
                dve.wait_ge(s["rt"], 8 * k + 7)
                dve.scalar_tensor_tensor(oh[:], iota, topf[:, 1:2], oh[:], ALU.is_equal, ALU.add).then_inc(s["rt"], 1)
                dve.wait_ge(s["rt"], 8 * k + 8)
                if later:
                    dve.wait_ge(s["y_ps"], k)
                dve.tensor_tensor(comb[:, 0:E], oh[:], sc[:], ALU.mult).then_inc(s["comb_done"], 1)
                dve.wait_ge(s["comb_done"], k + 1)
                for e in range(NE):
                    dve.wait_ge(s["silu_done"], NE * k + e + 1)
                    if e >= 2:
                        dve.wait_ge(s["hT_ps"], NE * k + e - 1)
                    dve.scalar_tensor_tensor(h[e % 2][:], ps[:, 2 + e % 2, INTER:2 * INTER], comb[:, e:e + 1], hs[e % 2][:],
                                             ALU.mult, ALU.mult).then_inc(s["h_done"], 1)
                dve.wait_ge(s["y_ps"], k + 1)
                dve.tensor_tensor(xall[:, bass.ds(k, 1), :], ps[:, 6, 0:D].unsqueeze(1), xall[:, bass.ds(k, 1), :], ALU.add
                                  ).then_inc(s["y_done"], 1)

            over_tiles(dve, tile)

        def moe_pool(pool):
            pool.wait_ge(s["x3_done"], 2 * B)
            def tile(k, later):
                apart(pool, "ln3_aggr", k + 1)
                pool.tensor_scalar(rstd[:, 0, 0:1], mv[:, 0, 1:2], EPS, None, ALU.add).then_inc(s["ln3_eps"], 1)
                pool.wait_ge(s["ln3_eps"], k + 1)
                pool.tensor_tensor(rstd[:, 1, 0:1], rstd[:, 0, 0:1], half[:, 0:1], ALU.pow).then_inc(s["ln3_rstd"], 1)
                apart(pool, "xn3T_sb", k + 1)
                if later:
                    apart(pool, "y_ps", k)
                pool.tensor_copy(x3_hi[:], xn3T[:]).then_inc(s["xT_split"], 1)
                pool.wait_ge(s["xT_split"], 2 * k + 1)
                pool.tensor_tensor(x3_lo[:], xn3T[:], x3_hi[:].bitcast(F32), ALU.subtract).then_inc(s["xT_split"], 1)

            over_tiles(pool, tile)

        block = stack.enter_context(nc.Block())

        def phases(eng, step):
            step(0, True, False)
            with eng.Fori(1, B) as i:
                step(i, True, True)
            step(B, False, True)

        @block.sync
        def _(sp):
            sp.dma_start(cst[:], consts).then_inc(s["consts_in"], 16)
            xt = x.rearrange("b (t p) d -> p (b t) d", p=P)
            sp.dma_start(xall[:, 0:T, :], xt[:, 0:T, :]).then_inc(s["x_first_in"], 16)
            for dst, src in ((wq_sb, wq), (wk_sb, wk), (wv_sb, wv), (wr_sb, wr), (wx_sb, wx), (gate_sb, gate)):
                sp.dma_start(dst[:], src).then_inc(s["weights_in"], 16)
            sp.dma_start(infoT[:], ctxT[0]).then_inc(s["infoT_in"], 16)
            sp.dma_start(xall[:, T:NT, :], xt[:, T:NT, :]).then_inc(s["x_in"], 16)
            sp.dma_start(w2_sb[:], w2).then_inc(s["weights_in"], 16)

            def step(i, new, old):
                if not new:
                    return
                if old:
                    apart(sp, "info_hi_done", 2 * i)
                    apart(sp, "info_lo_done", i)
                    sp.dma_start(infoT[:], ctxT[bass.ds(i, 1)].rearrange("o d m -> (o d) m")).then_inc(s["infoT_in"], 16)
                apart(sp, "parts_done", 3 * i + 3)
                for z in range(2):
                    for a in range(HA):
                        sp.dma_start(dq[z, a].rearrange("c p t -> p c t"), parts[64 * a:64 * a + 64, :, z, :]
                                     ).then_inc(s["parts_out"], 16)
                apart(sp, "parts_out", 64 * i + 64)
                if old:
                    apart(sp, "gamma_ps", NG * i)
                rows = dq.rearrange("z a c (e g) t -> z a (c e) (g t)", e=HE)
                for a in range(HA):
                    r = 64 * a
                    for n in (3, 2, 1):
                        sp.dma_start(qst[r:r + n * HE].rearrange("r g t -> r (g t)"), rows[0, a, 0:n * HE]
                                     ).then_inc(s["stack_in"], 16)
                        for m in range(n):
                            sp.dma_start(kst[r + m * HE:r + (m + 1) * HE].rearrange("r g t -> r (g t)"),
                                         rows[1, a, (3 - n) * HE:(4 - n) * HE]).then_inc(s["stack_in"], 16)
                        r += n * HE
                apart(sp, "msplit_step", 4 * i + 4)
                sp.dma_start(dm.rearrange("c h t -> h c t"), mparts[:]).then_inc(s["mparts_out"], 16)
                apart(sp, "mparts_out", 16 * i + 16)
                for a in range(HA):
                    sp.dma_start(qst[64 * a + QROWS:64 * a + KROWS].rearrange("r g t -> r (g t)"),
                                 dm[:, a * HG:(a + 1) * HG, :].rearrange("c g t -> c (g t)")
                                 ).then_inc(s["mrows_in"], 16)
                if old:
                    apart(sp, "xpv_ps", 2 * i)
                sp.dma_start(info[:, 0:MB, :], ctx[bass.ds(i, 1), 0:MF, :].rearrange("o (m p) d -> p (o m) d", p=P)
                             ).then_inc(s["info_in"], 16)
                sp.dma_start(info[0:MR, MB, :], ctx[bass.ds(i, 1), MF:M, :].rearrange("o p d -> (o p) d")
                             ).then_inc(s["info_in"], 16)

            phases(sp, step)
            out_tiles = out.rearrange("b (t p) d -> p (b t) d", p=P)
            sp.wait_ge(s["y_done"], NT)
            sp.dma_start(out_tiles, xall[:]).then_inc(s["x_in"], 16)
            sp.wait_ge(s["x_in"], 32)

        @block.tensor
        def _(pe):
            pe.wait_ge(s["consts_in"], 16)
            pe.wait_ge(s["weights_in"], 16 * 7)
            pe.wait_ge(s["const_done"], 2)

            def transposed(old_t, out_ps, src):
                return pe.transpose(out_ps, src, ident[0:src.shape[0], 0:src.shape[0]])

            def step(i, new, old):
                j = i - 1
                if old:
                    pe.wait_ge(s["oT_sb"], 2 * j + 2)
                    pe.wait_ge(s["p_exp"], NG * j + NG)
                    for t in range(T):
                        for n in range(NG):
                            mm = pe.transpose(ps[:, t, n * P:(n + 1) * P], oT[:, n, t * P:(t + 1) * P], ident)
                    mm.then_inc(s["o_ps"], 1)
                if new:
                    pe.wait_ge(s["xn1_done"], 2 * i + 2)
                    if old:
                        pe.wait_ge(s["oT_sb"], 2 * j + 2)
                    for t in range(T):
                        mm = pe.transpose(ps[:, 6, t * P:(t + 1) * P], xn1[:, t, :], ident)
                    mm.then_inc(s["xn1T_ps"], 1)
                if old:
                    pe.wait_ge(s["on_done"], j + 1)
                    for t in range(T):
                        mm = pe.transpose(ps[:, 2, t * P:(t + 1) * P], on[:, t, :], ident)
                    mm.then_inc(s["onT_ps"], 1)
                if new:
                    pe.wait_ge(s["xn1T_sb"], i + 1)
                    pe.matmul(ps[:, 7, 0:S], lhsT=wq_sb[:], rhs=xn1T[:], start=True, stop=True)
                    pe.matmul(ps[:, 7, S:2 * S], lhsT=wk_sb[:], rhs=xn1T[:], start=True, stop=True).then_inc(s["qk_ps"], 1)
                    for t in range(T):
                        mm = pe.matmul(ps[:, 6, S + t * P:S + (t + 1) * P], lhsT=xn1T[:, t * P:(t + 1) * P], rhs=wv_sb[:],
                                       start=True, stop=True)
                    mm.then_inc(s["v_ps"], 1)
                if old:
                    pe.wait_ge(s["onT_sb"], j + 1)
                    for t in range(T):
                        mm = pe.matmul(ps[:, 3, t * P:(t + 1) * P], lhsT=onT[:, t * P:(t + 1) * P], rhs=wr_sb[:],
                                       start=True, stop=True)
                    mm.then_inc(s["wr_ps"], 1)
                if new:
                    pe.wait_ge(s["v_done"], i + 1)
                    def v_of(t):
                        return vaug[:, t, :, 0:HE]
                    pe.matmul(ps[:, 6, 0:P], lhsT=upper, rhs=v_of(0), start=True, stop=False)
                    pe.matmul(ps[:, 6, 0:P], lhsT=ones, rhs=v_of(1), start=False, stop=True)
                    pe.matmul(ps[:, 6, P:S], lhsT=upper, rhs=v_of(1), start=True, stop=True).then_inc(s["sv_ps"], 1)
                if old:
                    pe.wait_ge(s["xn2_done"], 2 * j + 2)
                    for t in range(T):
                        mm = pe.transpose(ps[:, 2, S + t * P:S + (t + 1) * P], xn2[:, t, :], ident)
                    mm.then_inc(s["xn2T_ps"], 1)
                    pe.wait_ge(s["xn2T_sb"], j + 1)
                    pe.matmul(ps[:, 3, S:2 * S], lhsT=wx_sb[:], rhs=xn2T[:], start=True, stop=True).then_inc(s["q2_ps"], 1)

                def cross_scores(t):
                    if t == 0:
                        pe.wait_ge(s["q2_lo_done"], j + 1)
                        pe.wait_ge(s["info_lo_done"], j + 1)
                    else:
                        pe.wait_ge(s["xexp_done"], 2 * j + 1)
                    for c in range(MF // 512):
                        cols = slice(c * 512, (c + 1) * 512)
                        for n, (a, b) in enumerate(((q2_hi, info_hi), (q2_hi, info_lo), (q2_lo, info_hi))):
                            pe.matmul(ps[:, c, :], lhsT=a[:, t * P:(t + 1) * P], rhs=b[:, cols], start=(n == 0), stop=(n == 2))
                    pe.matmul(ps[:, 3, 0:MR], lhsT=q2[:, t * P:(t + 1) * P], rhs=info_tail[:], start=True, stop=True
                              ).then_inc(s["xs_ps"], 1)

                def cross_values(t, blocks):
                    for q in blocks:
                        n = 4 * t + q
                        if q == 0:
                            pe.wait_ge(s["xexp_done"], 2 * j + t + 1)
                        if n >= 2:
                            pe.wait_ge(s["xt_act"] if n % 2 == 0 else s["xt_dve"], 4 * j + n // 2)
                        elif n == 1 and new:
                            pe.wait_ge(s["mT_sb"], i + 1)
                        elif n == 0 and new:
                            pe.wait_ge(s["sv_sb"], i + 1)
                        for m in range(4 * q, min(4 * q + 4, NB)):
                            w = P if m < MB else MR
                            mm = pe.transpose(ps[0:w, 6 + n % 2, (m % 4) * P:(m % 4 + 1) * P],
                                              xprob[t][:, m * P:m * P + w], ident)
                        mm.then_inc(s["xt_ps"], 1)
                    for q in blocks:
                        n = 4 * t + q
                        if q == 0 and t == 0:
                            pe.wait_ge(s["info_in"], 32 * j + 32)
                            if new:
                                pe.wait_ge(s["alpha_max"], 12 * i + 12)
                        pe.wait_ge(s["xt_act"] if n % 2 == 0 else s["xt_dve"], 4 * j + n // 2 + 1)
                        for m in range(4 * q, min(4 * q + 4, NB)):
                            w = P if m < MB else MR
                            mm = pe.matmul(ps[:, 4 + t, 0:D], lhsT=xprobT[t][0:w, m, :], rhs=info[0:w, m, :],
                                           start=(m == 0), stop=(m == NB - 1))
                    if blocks[-1] == 3:
                        mm.then_inc(s["xpv_ps"], 1)

                if old:
                    cross_scores(0)
                if new:
                    pe.wait_ge(s["stack_in"], 16 * 18 * i + 16 * 18)
                    u = 0
                    for n in range(NG):
                        a, g0 = n // 2, 4 * (n % 2)
                        r = slice(64 * a, 64 * a + QROWS)
                        for kind in range(3):
                            if u >= 2:
                                pe.wait_ge(s["alpha_max"], 12 * i + u - 1)
                            bank = ps[:, 4 + u % 2, :]
                            if kind == 0:
                                for c in range(4):
                                    pe.matmul(bank[:, c * P:(c + 1) * P], lhsT=qst[r, g0 + c, 0:P], rhs=kst[r, g0 + c, 0:P],
                                              start=(c == 0), stop=False, skip_group_check=True)
                                mm = pe.matmul(bank, lhsT=ident_bf[:], rhs=mask_bf[:].rearrange("p a b -> p (a b)"),
                                               start=False, stop=True, skip_group_check=True)
                            else:
                                for c in range(2):
                                    g = g0 + 2 * (kind - 1) + c
                                    pe.matmul(bank[:, c * S:(c + 1) * S], lhsT=qst[r, g, P:S], rhs=kst[r, g, :],
                                              start=(c == 0), stop=False, skip_group_check=True)
                                mm = pe.matmul(bank.rearrange("p (c n) -> p c n", c=2)[:, :, P:S], lhsT=ident_bf[:],
                                               rhs=mask_bf[:, 0:2, :], start=False, stop=True, skip_group_check=True)
                            mm.then_inc(s["alpha_ps"], 1)
                            u += 1
                    pe.wait_ge(s["negm_done"], i + 1)
                    pe.wait_ge(s["qk_sb"], 2 * i + 2)
                    for t in range(T):
                        mm = pe.transpose(ps[0:H, 7, t * P:(t + 1) * P], negm[:, t, :], ident)
                    mm.then_inc(s["mT_ps"], 1)
                if old:
                    cross_values(0, (0, 1))
                    cross_scores(1)
                    cross_values(0, (2, 3))
                    cross_values(1, (0, 1))
                    cross_values(1, (2, 3))
                if new:
                    pe.wait_ge(s["mrows_in"], 32 * i + 32)
                    if old:
                        pe.wait_ge(s["xexp_done"], 2 * j + 2)

                    def gamma(n):
                        if n >= 2:
                            pe.wait_ge(s["p_exp"], NG * i + n - 1)
                        elif n == 1 and old:
                            pe.wait_ge(s["x3_done"], 2 * j + 2)
                        a, g0 = n // 2, 4 * (n % 2)
                        r = slice(64 * a, 64 * a + KROWS)
                        b0 = 3 * (n % 2)
                        for c in range(4):
                            pe.matmul(ps[:, b0 + c // 2, (c % 2) * S:(c % 2 + 1) * S], lhsT=kst[r, g0 + c, 0:P],
                                      rhs=qst[r, g0 + c, :], start=True, stop=True)
                        for c in range(4):
                            mm = pe.matmul(ps[:, b0 + 2, c * P:(c + 1) * P], lhsT=kst[r, g0 + c, P:S],
                                           rhs=qst[r, g0 + c, P:S], start=True, stop=True)
                        mm.then_inc(s["gamma_ps"], 1)

                    def values(n):
                        pe.wait_ge(s["p_masked"], 2 * (NG * i + n) + 2)
                        if old and n == 0:
                            pe.wait_ge(s["xt_act"], 4 * j + 4)
                            pe.wait_ge(s["xt_dve"], 4 * j + 4)
                        if not old and n == 0:
                            pe.wait_ge(s["sv_sb"], i + 1)
                            pe.wait_ge(s["mT_sb"], i + 1)
                        o = ps[:, 6 + n // 2, (n % 2) * S:(n % 2 + 1) * S]
                        for c in range(4):
                            pe.matmul(o[32 * c:32 * c + 32, :], lhsT=vaug[:, 0, 4 * n + c, :],
                                      rhs=prob[n % 2][:, c * S:(c + 1) * S], start=True, stop=False, skip_group_check=True)
                        for c in range(4):
                            mm = pe.matmul(o[32 * c:32 * c + 32, P:S], lhsT=vaug[:, 1, 4 * n + c, :],
                                           rhs=prob[n % 2][:, 4 * S + c * P:4 * S + (c + 1) * P], start=False, stop=True,
                                           skip_group_check=True)
                        mm.then_inc(s["pv_ps"], 1)

                    gamma(0)
                    for n in range(NG):
                        if n + 1 < NG:
                            gamma(n + 1)
                        values(n)

            phases(pe, step)
            moe_pe(pe)

        @block.scalar
        def _(act):
            act.wait_ge(s["consts_in"], 16)

            def step(i, new, old):
                j = i - 1
                if new:
                    act.wait_ge(s["xn1T_ps"], i + 1)
                    act.copy(xn1T[:], ps[:, 6, 0:S]).then_inc(s["xn1T_sb"], 1)
                if old:
                    act.wait_ge(s["onT_ps"], j + 1)
                    act.copy(onT[:], ps[:, 2, 0:S]).then_inc(s["onT_sb"], 1)
                if new:
                    act.wait_ge(s["qk_ps"], i + 1)
                    if old:
                        act.wait_ge(s["parts_done"], 3 * i)
                    for z in range(2):
                        act.activation(qk[:, z, :], ps[:, 7, z * S:(z + 1) * S], ACT.Identity,
                                       bias=cst[:, C_BIAS + z:C_BIAS + z + 1]).then_inc(s["qk_sb"], 1)
                    act.wait_ge(s["sv_ps"], i + 1)
                    if old:
                        act.wait_ge(s["emsv_done"], i)
                    act.copy(sv[:].rearrange("p t d -> p (t d)"), ps[:, 6, 0:S]).then_inc(s["sv_sb"], 1)
                if old:
                    act.wait_ge(s["xn2T_ps"], j + 1)
                    act.copy(xn2T[:], ps[:, 2, S:2 * S]).then_inc(s["xn2T_sb"], 1)
                    act.wait_ge(s["q2_ps"], j + 1)
                    act.activation(q2[:], ps[:, 3, S:2 * S], ACT.Identity, bias=cst[:, C_BIAS + 2:C_BIAS + 3]
                                   ).then_inc(s["q2_sb"], 1)

                def cross_exp(t):
                    act.wait_ge(s["xmax_done"], 2 * j + t + 1)
                    act.activation(xprob[t][:], flat(0, M), ACT.Exp, bias=xmax[:, t:t + 1], accum_out=xsum[:, t:t + 1]
                                   ).then_inc(s["xexp_done"], 1)

                def cross_copy(t, q):
                    n = 4 * t + q
                    act.wait_ge(s["xt_ps"], 8 * j + n + 1)
                    m1 = min(4 * q + 4, NB)
                    w = P if m1 <= MB else MR
                    act.copy(xprobT[t][0:w, 4 * q:m1, :], ps[0:w, 6, 0:(m1 - 4 * q) * P].rearrange("p (m n) -> p m n", n=P)
                             ).then_inc(s["xt_act"], 1)

                if old:
                    cross_exp(0)
                if new:
                    act.wait_ge(s["negm_done"], i + 1)
                    act.activation(em[:], negm[:], ACT.Exp, scale=SCALE).then_inc(s["em_done"], 1)
                    act.wait_ge(s["mT_ps"], i + 1)
                    act.copy(mT[:], ps[0:H, 7, 0:S]).then_inc(s["mT_sb"], 1)
                if old:
                    cross_copy(0, 0)
                    cross_exp(1)
                    cross_copy(0, 2)
                    cross_copy(1, 0)
                    cross_copy(1, 2)
                if new:
                    for n in range(NG):
                        act.wait_ge(s["gamma_ps"], NG * i + n + 1)
                        if n >= 2:
                            act.wait_ge(s["pv_ps"], NG * i + n - 1)
                        act.activation(prob[n % 2][:], flat(3 * (n % 2), 3 * 512), ACT.Exp, scale=SCALE).then_inc(s["p_exp"], 1)

            phases(act, step)
            moe_act(act)

        @block.vector
        def _(dve):
            dve.wait_ge(s["consts_in"], 16)
            dve.tensor_copy(ident_bf[:], ident).then_inc(s["const_done"], 1)
            dve.tensor_copy(mask_bf[:], cst[:, C_MASK:C_MASK + P].unsqueeze(1).to_broadcast([P, NG, P])).then_inc(s["const_done"], 1)
            dve.memset(vaug[:], 1.0)
            dve.memset(kst[:], 1.0).then_inc(s["const_done"], 1)
            dve.wait_ge(s["const_done"], 3)

            def normalised(b, mvt, r, dst, rs, done, k):
                dve.wait_ge(s[rs], k)
                for t in range(T):
                    dve.tensor_scalar(dst[:, t:t + 1, :], xall[:, bass.ds(2 * b + t, 1), :], mvt[:, t, 0:1], r[:, 1, t:t + 1],
                                      ALU.subtract, ALU.mult).then_inc(s[done], 1)

            def step(i, new, old):
                j = i - 1
                if old:
                    dve.wait_ge(s["o_ps"], j + 1)
                    dve.wait_ge(s["emc_done"], j + 1)
                    dve.wait_ge(s["emsv_done"], j + 1)
                    o = ps[:, 0:T, :].rearrange("p t (h e) -> p t h e", e=32)
                    dve.tensor_tensor(den[:], o[:, :, :, HE], emc[:], ALU.add).then_inc(s["den_done"], 1)
                    dve.tensor_tensor(num[:].rearrange("p t (h e) -> p t h e", e=HE), o[:, :, :, 0:HE],
                                      emsv[:].rearrange("p t (h e) -> p t h e", e=HE), ALU.add).then_inc(s["num_done"], 1)
                    dve.wait_ge(s["den_done"], j + 1)
                    dve.reciprocal(rden[:], den[:]).then_inc(s["rden_done"], 1)
                if new:
                    if not old:
                        apart(dve, "x_first_in", 16)
                    else:
                        apart(dve, "x_in", 16)
                    for t in range(T):
                        dve.bn_stats(st[:, t, :], xall[:, bass.ds(2 * i + t, 1), :]).then_inc(s["ln1_stats"], 1)
                    apart(dve, "ln1_stats", 2 * i + 2)
                    for t in range(T):
                        dve.bn_aggr(mv[:, t, :], st[:, t, :]).then_inc(s["ln1_aggr"], 1)
                    normalised(i, mv, rstd, xn1, "ln1_rstd", "xn1_done", i + 1)
                if new:
                    dve.wait_ge(s["v_ps"], i + 1)
                    dve.tensor_tensor(vaug[:, :, :, 0:HE], ps[:, 6, S:2 * S].rearrange("p (t h e) -> p t h e", t=T, e=HE),
                                      cst[:, C_BV:C_BV + D].rearrange("p (h e) -> p h e", e=HE).unsqueeze(1).to_broadcast([P, T, H, HE]),
                                      ALU.add).then_inc(s["v_done"], 1)
                if old:
                    dve.wait_ge(s["wr_ps"], j + 1)
                    dve.wait_ge(s["xb_done"], j + 1)
                    dve.tensor_tensor(xall[:, bass.ds(2 * j, T), :], ps[:, 3, 0:S].rearrange("p (t d) -> p t d", t=T), xb[:],
                                      ALU.add).then_inc(s["x2_done"], 1)
                    apart(dve, "x2_done", j + 1)
                    for t in range(T):
                        dve.bn_stats(st2[:, t, :], xall[:, bass.ds(2 * j + t, 1), :]).then_inc(s["ln2_stats"], 1)
                    apart(dve, "ln2_stats", 2 * j + 2)
                    for t in range(T):
                        dve.bn_aggr(mv2[:, t, :], st2[:, t, :]).then_inc(s["ln2_aggr"], 1)
                    normalised(j, mv2, rstd2, xn2, "ln2_rstd", "xn2_done", j + 1)

                def cross_max(t):
                    dve.wait_ge(s["xs_ps"], 2 * j + t + 1)
                    dve.tensor_reduce(xmax[:, t:t + 1], flat(0, M), AX.X, ALU.max, negate=True).then_inc(s["xmax_done"], 1)

                def cross_copy(t, q):
                    n = 4 * t + q
                    dve.wait_ge(s["xt_ps"], 8 * j + n + 1)
                    for m0, m1, w in (((4 * q, min(4 * q + 4, MB), P),) if q < 3 else ((MB, NB, MR),)):
                        dve.tensor_copy(xprobT[t][0:w, m0:m1, :], ps[0:w, 7, 0:(m1 - m0) * P].rearrange("p (m n) -> p m n", n=P)
                                        ).then_inc(s["xt_dve"], 1)

                def cross_out(t):
                    if t == 0:
                        dve.wait_ge(s["xexp_done"], 2 * j + 2)
                        dve.reciprocal(xrec[:], xsum[:]).then_inc(s["xrec_done"], 1)
                        dve.wait_ge(s["xrec_done"], j + 1)
                    dve.wait_ge(s["xpv_ps"], 2 * j + t + 1)
                    dve.scalar_tensor_tensor(xall[:, bass.ds(2 * j + t, 1), :], ps[:, 4 + t, 0:D].unsqueeze(1), xrec[:, t:t + 1],
                                             xall[:, bass.ds(2 * j + t, 1), :], ALU.mult, ALU.add).then_inc(s["x3_done"], 1)

                if old:
                    cross_max(0)
                if new:
                    u = 0
                    for n in range(NG):
                        for kind in range(3):
                            dve.wait_ge(s["alpha_ps"], 12 * i + u + 1)
                            bank = ps[:, 4 + u % 2, :]
                            if kind == 0:
                                dve.tensor_reduce(mx[:, 0, 4 * n:4 * n + 4], bank.rearrange("p (c n) -> p c n", c=4), AX.X,
                                                  ALU.max).then_inc(s["alpha_max"], 1)
                            else:
                                h = 4 * n + 2 * (kind - 1)
                                dve.tensor_reduce(mx[:, 1, h:h + 2], bank.rearrange("p (c n) -> p c n", c=2), AX.X,
                                                  ALU.max).then_inc(s["alpha_max"], 1)
                            u += 1
                    dve.wait_ge(s["alpha_max"], 12 * i + 12)
                    if old:
                        dve.wait_ge(s["em_done"], i)
                        dve.wait_ge(s["mT_ps"], i)
                    dve.tensor_scalar(negm[:], mx[:], 0.0, -1.0, ALU.max, ALU.mult).then_inc(s["negm_done"], 1)
                if old:
                    cross_copy(0, 1)
                    cross_max(1)
                    cross_copy(0, 3)
                    cross_copy(1, 1)
                    cross_copy(1, 3)
                    cross_out(0)
                    cross_out(1)
                if new:
                    for n in range(2):
                        dve.wait_ge(s["pv_ps"], NG * i + 2 * n + 2)
                        dve.tensor_copy(oT[:, 2 * n:2 * n + 2, :], ps[:, 6 + n, :].rearrange("p (n t) -> p n t", n=2)
                                        ).then_inc(s["oT_sb"], 1)

            phases(dve, step)
            moe_dve(dve)

        @block.gpsimd
        def _(pool):
            pool.memset(half[:], -0.5).then_inc(s["w13_step"], 1)
            pool.wait_ge(s["consts_in"], 16)
            for e in range(NE):
                if e:
                    pool.wait_ge(s["w13_step"], 2 * e + 1)
                pool.dma_start(w13_raw[:], w13[e]).then_inc(s["w13_in"], 16)
                apart(pool, "w13_in", 16 * e + 16)
                pool.tensor_copy(w13_hi[:, e, :], w13_raw[:]).then_inc(s["w13_step"], 1)
                pool.wait_ge(s["w13_step"], 2 * e + 2)
                pool.tensor_tensor(w13_lo[:, e, :], w13_raw[:], w13_hi[:, e, :].bitcast(F32), ALU.subtract).then_inc(s["w13_step"], 1)

            def inverse_deviation(mvt, r, aggr, eps, rs, k):
                apart(pool, aggr, 2 * k)
                pool.tensor_scalar(r[:, 0, :], mvt[:, :, 1], EPS, None, ALU.add).then_inc(s[eps], 1)
                pool.wait_ge(s[eps], k)
                pool.tensor_tensor(r[:, 1, :], r[:, 0, :], half[:, 0:T], ALU.pow).then_inc(s[rs], 1)

            def step(i, new, old):
                j = i - 1
                if old:
                    pool.wait_ge(s["rden_done"], j + 1)
                    pool.wait_ge(s["num_done"], j + 1)
                    pool.tensor_tensor(on[:].rearrange("p t (h e) -> p (t h) e", e=HE), num[:].rearrange("p t (h e) -> p (t h) e", e=HE),
                                       rden[:].rearrange("p t h -> p (t h)").unsqueeze(2).to_broadcast([P, T * H, HE]), ALU.mult
                                       ).then_inc(s["on_done"], 1)
                if new:
                    inverse_deviation(mv, rstd, "ln1_aggr", "ln1_eps", "ln1_rstd", i + 1)
                    apart(pool, "qk_sb", 2 * i + 2)
                    if old:
                        apart(pool, "parts_out", 64 * i)
                    flatp = parts[:].rearrange("p c z t -> p c (z t)")
                    flatq, flatr = qk[:].rearrange("p z t -> p (z t)"), qk_r[:].rearrange("p z t -> p (z t)")
                    pool.tensor_copy(flatp[:, 0], flatq).then_inc(s["parts_done"], 1)
                    pool.wait_ge(s["parts_done"], 3 * i + 1)
                    pool.tensor_tensor(flatr, flatq, flatp[:, 0], ALU.subtract).then_inc(s["split_step"], 1)
                    apart(pool, "split_step", i + 1)
                    pool.tensor_copy(flatp[:, 1], flatr).then_inc(s["parts_done"], 1)
                    pool.wait_ge(s["parts_done"], 3 * i + 2)
                    pool.tensor_tensor(flatp[:, 2], flatr, flatp[:, 1], ALU.subtract).then_inc(s["parts_done"], 1)
                if old:
                    inverse_deviation(mv2, rstd2, "ln2_aggr", "ln2_eps", "ln2_rstd", j + 1)
                if new:
                    pool.tensor_tensor(xb[:], xall[:, bass.ds(2 * i, T), :],
                                       cst[:, C_BR:C_BR + D].unsqueeze(1).to_broadcast([P, T, D]), ALU.add).then_inc(s["xb_done"], 1)
                if old:
                    apart(pool, "q2_sb", j + 1)
                    pool.tensor_copy(q2_hi[:], q2[:]).then_inc(s["q2_hi_done"], 1)
                    pool.wait_ge(s["q2_hi_done"], j + 1)
                    pool.tensor_tensor(q2_lo[:], q2[:], q2_hi[:].bitcast(F32), ALU.subtract).then_inc(s["q2_lo_done"], 1)
                if new:
                    apart(pool, "mT_sb", i + 1)
                    if old:
                        apart(pool, "mparts_out", 16 * i)
                    pool.tensor_copy(mparts[:, 0], mT[:]).then_inc(s["msplit_step"], 1)
                    pool.wait_ge(s["msplit_step"], 4 * i + 1)
                    pool.tensor_tensor(mT_r[:], mT[:], mparts[:, 0], ALU.subtract).then_inc(s["msplit_step"], 1)
                    apart(pool, "msplit_step", 4 * i + 2)
                    pool.tensor_copy(mparts[:, 1], mT_r[:]).then_inc(s["msplit_step"], 1)
                    pool.wait_ge(s["msplit_step"], 4 * i + 3)
                    pool.tensor_tensor(mparts[:, 2], mT_r[:], mparts[:, 1], ALU.subtract).then_inc(s["msplit_step"], 1)
                    pool.wait_ge(s["em_done"], i + 1)
                    pool.tensor_tensor(emc[:].rearrange("p t h -> p (t h)"), em[:].rearrange("p t h -> p (t h)"), cst[:, C_CNT:C_CNT + T * H],
                                       ALU.mult).then_inc(s["emc_done"], 1)
                    pool.wait_ge(s["sv_sb"], i + 1)
                    pool.tensor_tensor(emsv[:].rearrange("p t (h e) -> p (t h) e", e=HE), sv[:].rearrange("p t (h e) -> p (t h) e", e=HE),
                                       em[:].rearrange("p t h -> p (t h)").unsqueeze(2).to_broadcast([P, T * H, HE]), ALU.mult
                                       ).then_inc(s["emsv_done"], 1)
                    for n in range(NG):
                        apart(pool, "p_exp", NG * i + n + 1)
                        for v in (prob[n % 2][:, 0:4 * S].rearrange("p (c q) -> p c q", c=4)[:, :, 0:P],
                                  prob[n % 2][:, 4 * S:].rearrange("p (c q) -> p c q", c=4)):
                            pool.affine_select(out=v, in_=v, compare_op=ALU.is_gt, fill=0.0, base=0, pattern=[[0, 4], [1, P]],
                                               channel_multiplier=-1).then_inc(s["p_masked"], 1)
                    apart(pool, "infoT_in", 16 * i + 16)
                    if old:
                        apart(pool, "xs_ps", 2 * i)
                    pool.tensor_copy(info_hi[:], infoT[:, 0:MF]).then_inc(s["info_hi_done"], 1)
                    pool.tensor_copy(info_tail[:], infoT[:, MF:M]).then_inc(s["info_hi_done"], 1)
                    pool.wait_ge(s["info_hi_done"], 2 * i + 2)
                    pool.tensor_tensor(info_lo[:], infoT[:, 0:MF], info_hi[:].bitcast(F32), ALU.subtract).then_inc(s["info_lo_done"], 1)

            phases(pool, step)
            moe_pool(pool)



def constants(bv, br, bq, bk, bx, gate_bias):
    c = np.zeros((P, C_END), np.float32)
    q, k = np.arange(P)[:, None], np.arange(P)[None, :]
    c[:, C_ID:C_ID + P] = q == k
    c[:, C_MASK:C_MASK + P] = np.where(k >= q, np.float32(NEG), np.float32(0))
    c[:, C_U:C_U + P] = q >= k
    c[:, C_ONE:C_ONE + P] = 1
    for t in range(T):
        c[:, C_CNT + t * H:C_CNT + (t + 1) * H] = S - (t * P + q)
    c[:, C_BV:C_BV + D] = bv
    c[:, C_BR:C_BR + D] = br
    c[:, C_BIAS], c[:, C_BIAS + 1], c[:, C_BIAS + 2] = bq, bk, bx
    c[:, C_GB:C_GB + E] = gate_bias
    c[:, C_IOTA:C_IOTA + E] = np.arange(E)
    return c


def kernel(**inputs):
    import concourse.bacc as bacc
    from concourse.bass_utils import run_bass_kernel_spmd

    a = {n: np.asarray(v) for n, v in inputs.items()}
    wqkv, bqkv = a["L0_attn_Wqkv"], a["L0_attn_bqkv"]
    heads = np.arange(H)
    wq, wk, wv = (np.zeros((P, P), np.float32) for _ in range(3))
    for h in heads:
        rows = slice(h * HE, (h + 1) * HE)
        col = (h // HG) * 64 + np.arange(HE) * HG + h % HG
        wq[rows, col] = wqkv[:, 0:HE]
        wk[rows, col] = wqkv[:, HE:2 * HE]
        wv[rows, rows] = wqkv[:, 2 * HE:]
    order = lambda b: np.tile(np.repeat(b, HG), HA)
    consts = constants(np.tile(bqkv[2 * HE:], H), a["L0_attn_br"], order(bqkv[0:HE]), order(bqkv[HE:2 * HE]), a["L0_xattn_b"],
                       a["L0_ffn_gate_bias"])
    w1 = np.concatenate([a["L0_ffn_w1"], a["L0_ffn_sw1"][None]])
    w3 = np.concatenate([a["L0_ffn_w3"], a["L0_ffn_sw3"][None]])
    w2 = np.concatenate([a["L0_ffn_w2"], a["L0_ffn_sw2"][None]])
    arrays = {
        "x": a["x"], "ctx": a["ctx_1024"], "ctxT": a["ctx_1024"].transpose(0, 2, 1), "consts": consts,
        "wq": wq, "wk": wk, "wv": wv, "wr": a["L0_attn_Wr"], "wx": a["L0_xattn_W"].T, "gate": a["L0_ffn_gate_w"].T,
        "w13": np.concatenate([w1, w3], axis=1).transpose(0, 2, 1),
        "w2": w2.reshape(NE, D, INTER // P, P).transpose(3, 0, 2, 1),
    }
    arrays = {f"in_{n}": np.ascontiguousarray(v) for n, v in arrays.items()}
    nc = bacc.Bacc("TRN2", target_bir_lowering=False, num_devices=1)
    args = [nc.dram_tensor(n, v.shape, mybir.dt.from_np(v.dtype), kind="ExternalInput").ap() for n, v in arrays.items()]
    out = nc.dram_tensor("out", (B, S, D), F32, kind="ExternalOutput").ap()
    decoder_kernel(nc, *args, out)
    r = run_bass_kernel_spmd(nc, [arrays], core_ids=[0])
    return r.results[0]["out"]
```

```python
from contextlib import ExitStack

import numpy as np
import concourse.bass as bass
from concourse import mybir

ALU = mybir.AluOpType
ACT = mybir.ActivationFunctionType
AX = mybir.AxisListType
F32 = mybir.dt.float32
F32R = mybir.dt.float32r
BF16 = mybir.dt.bfloat16
U32 = mybir.dt.uint32

P = 128
B, S, D = 16, 256, 128
T = S // P
NT = B * T
H = 16
HE = D // H
HA = 2
HG = H // HA
NG = 4
M = 1601
MB = M // P
MR = M - MB * P
MF = MB * P
NB = MB + 1
H0 = 7 * P
MF3 = H0 + 512
TAIL = M - MF3
HW = (H0, M - H0)
E = 8
INTER = 256
GT = 4
GN = GT * P
NGR = NT // GT
NE = E + 1
WS = NE * 2 * INTER // B
EPS = 1e-5
SCALE = float(1.0 / np.sqrt(np.float32(HE)))
NEG = -1.0e30
QROWS = 48
KROWS = 51

C_ID, C_MASK, C_U, C_ONE, C_CNT, C_BV, C_BR, C_BIAS, C_GB, C_IOTA, C_END = 0, 128, 256, 384, 512, 544, 672, 800, 804, 812, 820


def decoder_kernel(nc, x, ctx, ctxT, consts, wq, wk, wv, wr, wx, gate, w13, w2, out):
    with ExitStack() as stack:
        def sb(name, shape, dt=F32):
            return stack.enter_context(nc.sbuf_tensor(name, shape, dt))

        def sem(name):
            return stack.enter_context(nc.semaphore(name))

        ps = stack.enter_context(nc.psum_tensor("banks", [P, 8, 512], F32))

        dq = nc.dram_tensor("stack_parts", [2, HA, 3, P // HA, S], BF16).ap()
        dm = nc.dram_tensor("max_parts", [3, H, S], BF16).ap()

        cst = sb("cst", [P, C_END])
        ident_bf = sb("ident_bf", [P, P], BF16)
        mask_bf = sb("mask_bf", [P, NG, P], BF16)
        half = sb("half", [P, 2 * T])
        wq_sb, wk_sb, wv_sb = sb("wq_sb", [P, P]), sb("wk_sb", [P, P]), sb("wv_sb", [P, P])
        wr_sb, wx_sb = sb("wr_sb", [P, P]), sb("wx_sb", [P, P])
        gate_sb = sb("gate_sb", [P, E])
        w13_raw = sb("w13_raw", [P, WS])
        w13_hi = sb("w13_hi", [P, NE, 2 * INTER], F32R)
        w13_lo = sb("w13_lo", [P, NE, 2 * INTER], F32R)
        w2_sb = sb("w2_sb", [P, NE, INTER // P, D])
        ident = cst[:, C_ID:C_ID + P]
        upper = cst[:, C_U:C_U + P]
        ones = cst[:, C_ONE:C_ONE + P]

        xall = sb("xall", [P, NT, D])

        st = sb("st", [P, T, 6])
        mv = sb("mv", [P, T, 2])
        rstd = sb("rstd", [P, 2, T])
        xn1, xn2 = sb("xn1", [P, T, D]), sb("xn2", [P, T, D])
        xb = sb("xb", [P, T, D])
        xn1T, xn2T = sb("xn1T", [P, S]), sb("xn2T", [P, S])
        st2 = sb("st2", [P, T, 6])
        mv2 = sb("mv2", [P, T, 2])
        rstd2 = sb("rstd2", [P, 2, T])

        qk = sb("qk", [P, 2, S])
        qk_r = sb("qk_r", [P, 2, S])
        parts = sb("parts", [P, 3, 2, S], BF16)
        qst, kst = sb("qst", [P, HG, S], BF16), sb("kst", [P, HG, S], BF16)
        vaug = sb("vaug", [P, T, H, 32])
        mx = sb("mx", [P, T, H])
        negm = sb("negm", [P, T, H])
        em = sb("em", [P, T, H])
        emc = sb("emc", [P, T, H])
        mT = sb("mT", [H, S])
        mT_r = sb("mT_r", [H, S])
        mparts = sb("mparts", [H, 3, S], BF16)
        sv = sb("sv", [P, T, D])
        emsv = sb("emsv", [P, T, D])
        prob = [sb(f"prob{n}", [P, 3 * 512]) for n in range(2)]
        oT = sb("oT", [P, NG, S])
        den = sb("den", [P, T, H])
        rden = sb("rden", [P, T, H])
        num = sb("num", [P, T, D])
        on = sb("on", [P, T, D])
        onT = sb("onT", [P, S])

        q2 = sb("q2", [P, S])
        q2_hi, q2_lo = sb("q2_hi", [P, S], F32R), sb("q2_lo", [P, S], F32R)
        infoT = sb("infoT", [P, M])
        info_hi, info_lo = sb("info_hi", [P, MF3], F32R), sb("info_lo", [P, MF3], F32R)
        info_tail = sb("info_tail", [P, TAIL])
        info = sb("info", [P, NB, D])
        xprob = [sb(f"xprob{n}", [P, 7 * P]) for n in range(2)]
        xprobT = [sb(f"xprobT{n}", [P, 7, P]) for n in range(2)]
        xmax, xsum, xc, xcs, xw, xdiff = (sb(n, [P, 2 * T]) for n in ("xmax", "xsum", "xc", "xcs", "xw", "xdiff"))
        xmin, xden, xrec = (sb(n, [P, T]) for n in ("xmin", "xden", "xrec"))

        s = {n: sem(n) for n in (
            "consts_in", "weights_in", "x_first_in", "x_in", "const_done", "w13_in", "w13_raw_done", "w13_step",
            "ln1_stats", "ln1_aggr", "ln1_eps", "ln1_rstd", "xn1_done", "xb_done",
            "xn1T_ps", "xn1T_sb", "qk_ps", "v_ps", "qk_sb", "v_done",
            "split_step", "parts_done", "parts_out", "stack_in",
            "sv_ps", "sv_sb", "alpha_ps", "alpha_max", "max_clip", "negm_done", "mT_ps", "mT_sb",
            "msplit_step", "mparts_out", "mrows_in", "em_done", "emc_done", "emsv_done",
            "gamma_ps", "p_exp", "p_masked", "pv_ps", "oT_sb",
            "o_ps", "den_done", "rden_done", "num_done", "on_done", "onT_ps", "onT_sb", "wr_ps", "x2_done",
            "ln2_stats", "ln2_aggr", "ln2_eps", "ln2_rstd", "xn2_done", "xn2T_ps", "xn2T_sb", "q2_ps", "q2_sb", "q2_hi_done", "q2_lo_done",
            "infoT_in", "info_hi_done", "info_lo_done", "info_in",
            "xs_ps", "xmax_done", "xexp_done", "xt_ps", "xt_act", "xt_dve", "xpv_ps", "xrec_done", "x3_done",
            "half_done", "w2_in", "w13_hi_done", "w13_lo_done", "xt_sb", "xmin_done", "xdiff_done", "xc_done", "xw_step", "xden_done", "xw_done", "out_done")}

        def apart(eng, name, value):
            eng.wait_ge(s[name], value)
            eng.sem_inc(passed[eng.engine], 1)

        passed = {e.engine: sem(f"passed_{n}") for n, e in (("dve", nc.vector), ("pool", nc.gpsimd), ("sp", nc.sync))}

        def flat(b0, n):
            return ps[:].rearrange("p b n -> p (b n)")[:, b0 * 512:b0 * 512 + n]

        xn3 = xprob[0][:, 0:GN].rearrange("p (t d) -> p t d", t=GT)
        xn3T = xprob[1][:, 0:GN]
        x3_hi, x3_lo = sb("x3_hi", [P, NT * P], F32R), sb("x3_lo", [P, NT * P], F32R)
        st3, mv3, rstd3 = sb("st3", [P, GT, 6]), sb("mv3", [P, GT, 2]), sb("rstd3", [P, 2, GT])
        logit, ex, sc, biased, eq, oh1, oh2, comb = (sb(n, [P, NT, E]) for n in
                                                     ("logit", "ex", "sc", "biased", "eq", "oh1", "oh2", "comb"))
        lmax, esum, erec, m1, i1, m2, i2 = (sb(n, [P, NT]) for n in ("lmax", "esum", "erec", "m1", "i1", "m2", "i2"))
        comb_g = sb("comb_g", [P, GT, E])
        sil = [prob[z][:, 2 * GN:3 * GN] for z in range(2)]
        h = [[prob[n][:, z * GN:(z + 1) * GN] for z in range(2)] for n in range(2)]
        for n in ("ln3_stats", "ln3_aggr", "ln3_eps", "ln3_rstd", "xn3_done", "xn3T_ps", "xn3T_sb", "x3_lo_done", "lg_ps", "lg_sb",
                  "route", "ex_done", "comb_done", "comb_g_done",
                  "up_ps", "silu_done", "h_done", "y_ps", "shared_done", "acc_done"):
            s[n] = sem(n)

        def shared_pass(step):
            def run(eng):
                step(-1, False, True, False)
                step(0, True, True, False)
                with eng.Fori(1, NGR - 1) as g:
                    step(g, True, True, True)
                step(NGR - 1, True, False, True)
            return run

        def routed_pass(eng, group):
            group(0, False)
            with eng.Fori(1, NGR) as g:
                group(g, True)

        def moe_pe(pe):
            pe.wait_ge(s["w13_lo_done"], B)
            pe.wait_ge(s["w2_in"], 16)
            pe.wait_ge(s["x3_done"], 4 * B)
            pe.wait_ge(s["xt_sb"], 8 * B)
            pe.wait_ge(s["oT_sb"], 2 * B)
            pe.wait_ge(s["p_exp"], 12 * B)

            def up(u, g, e, later):
                for z in range(2):
                    if later:
                        pe.wait_ge(s["h_done"], 2 * u - 1 + z)
                    for half_w in range(2):
                        w = slice(half_w * INTER + z * P, half_w * INTER + (z + 1) * P)
                        for n, (a, b) in enumerate(((w13_hi, x3_hi), (w13_lo, x3_hi), (w13_hi, x3_lo))):
                            mm = pe.matmul(ps[:, 2 * z + half_w, :], lhsT=a[:, e, w], rhs=b[:, bass.ds(g * GN, GN)],
                                           start=(n == 0), stop=(n == 2))
                    mm.then_inc(s["up_ps"], 1)

            def down(u, e, n):
                pe.wait_ge(s["h_done"], 2 * u + 2)
                for t in range(GT):
                    for z in range(2):
                        mm = pe.matmul(ps[:, 6 + n, t * D:(t + 1) * D], lhsT=h[n][z][:, t * P:(t + 1) * P], rhs=w2_sb[:, e, z, :],
                                       start=(z == 0), stop=(z == 1))
                mm.then_inc(s["y_ps"], 1)

            def step(g, new, nxt, later):
                f = g + 1
                if new:
                    pe.wait_ge(s["x3_lo_done"], g + 1)
                    up(g, g, E, later)
                if nxt:
                    pe.wait_ge(s["xn3_done"], GT * f + GT)
                    if new:
                        pe.wait_ge(s["xn3T_sb"], 2 * f)
                    for t in range(GT):
                        mm = pe.transpose(ps[:, 4, t * P:(t + 1) * P], xn3[:, t, :], ident)
                    mm.then_inc(s["xn3T_ps"], 1)
                if new:
                    if later:
                        pe.wait_ge(s["shared_done"], g)
                    down(g, E, 0)
                if nxt:
                    pe.wait_ge(s["xn3T_sb"], 2 * f + 2)
                    if new:
                        pe.wait_ge(s["lg_sb"], f)
                    for t in range(GT):
                        mm = pe.matmul(ps[:, 5, t * E:(t + 1) * E], lhsT=xn3T[:, t * P:(t + 1) * P], rhs=gate_sb[:],
                                       start=True, stop=True)
                    mm.then_inc(s["lg_ps"], 1)

            shared_pass(step)(pe)

            def group(g, later):
                for e in range(E):
                    r = E * g + e
                    up(NGR + r, g, e, True)
                    if e == 0 and later or e >= 3:
                        pe.wait_ge(s["acc_done"], GT * (r - 2))
                    elif later:
                        pe.wait_ge(s["acc_done"], GT * (r - 2))
                    elif e == 1:
                        pe.wait_ge(s["shared_done"], NGR)
                    if e or later:
                        down(NGR + r - 1, (e - 1) % E, (e - 1) % 2)

            routed_pass(pe, group)
            pe.wait_ge(s["acc_done"], GT * (E * NGR - 2))
            down(NGR + E * NGR - 1, E - 1, 1)

        def moe_act(act):
            def silu(u, later):
                for z in range(2):
                    act.wait_ge(s["up_ps"], 2 * u + z + 1)
                    if later:
                        act.wait_ge(s["h_done"], 2 * u - 1 + z)
                    act.activation(sil[z], ps[:, 2 * z, :], ACT.Silu).then_inc(s["silu_done"], 1)

            def step(g, new, nxt, later):
                f = g + 1
                if new:
                    silu(g, later)
                if nxt:
                    act.wait_ge(s["xn3T_ps"], f + 1)
                    if new:
                        act.wait_ge(s["lg_ps"], f)
                        act.wait_ge(s["x3_lo_done"], f)
                    act.copy(xn3T, ps[:, 4, :]).then_inc(s["xn3T_sb"], 1)
                    act.copy(x3_hi[:, bass.ds(f * GN, GN)], ps[:, 4, :]).then_inc(s["xn3T_sb"], 1)

            act.wait_ge(s["pv_ps"], NG * B)
            act.wait_ge(s["xt_ps"], 8 * B)
            shared_pass(step)(act)
            act.wait_ge(s["route"], 2)
            act.activation(ex[:], biased[:], ACT.Exp).then_inc(s["ex_done"], 1)

            def group(g, later):
                for e in range(E):
                    silu(NGR + E * g + e, True)

            routed_pass(act, group)

        def moe_dve(dve):
            dve.wait_ge(s["xt_ps"], 8 * B)
            apart(dve, "x3_done", 4 * B)

            def hidden(u, n, read):
                if read is not None:
                    dve.wait_ge(s["y_ps"], read)
                for z in range(2):
                    dve.wait_ge(s["silu_done"], 2 * u + z + 1)
                    dve.tensor_tensor(h[n][z], ps[:, 2 * z + 1, :], sil[z], ALU.mult).then_inc(s["h_done"], 1)

            def step(g, new, nxt, later):
                f = g + 1
                if new:
                    hidden(g, 0, g if later else None)
                if nxt:
                    if new:
                        apart(dve, "xn3_done", GT * f)
                    for t in range(GT):
                        dve.bn_stats(st3[:, t, :], xall[:, bass.ds(GT * f + t, 1), :]).then_inc(s["ln3_stats"], 1)
                    apart(dve, "ln3_stats", GT * f + GT)
                    for t in range(GT):
                        dve.bn_aggr(mv3[:, t, :], st3[:, t, :]).then_inc(s["ln3_aggr"], 1)
                if nxt:
                    dve.wait_ge(s["ln3_rstd"], f + 1)
                    if new:
                        dve.wait_ge(s["xn3T_ps"], f)
                    for t in range(GT):
                        dve.tensor_scalar(xn3[:, t:t + 1, :], xall[:, bass.ds(GT * f + t, 1), :], mv3[:, t, 0:1], rstd3[:, 1, t:t + 1],
                                          ALU.subtract, ALU.mult).then_inc(s["xn3_done"], 1)
                if new:
                    dve.wait_ge(s["y_ps"], g + 1)
                    xg = xall[:, bass.ds(GT * g, GT), :]
                    dve.tensor_tensor(xg, ps[:, 6, :].rearrange("p (t d) -> p t d", t=GT), xg, ALU.add).then_inc(s["shared_done"], 1)
                if nxt:
                    dve.wait_ge(s["lg_ps"], f + 1)
                    dve.tensor_copy(logit[:, bass.ds(GT * f, GT), :], ps[:, 5, 0:GT * E].rearrange("p (t e) -> p t e", t=GT)
                                    ).then_inc(s["lg_sb"], 1)

            shared_pass(step)(dve)

            count = iter(range(1, 100))

            def route(ins):
                ins.then_inc(s["route"], 1)
                dve.wait_ge(s["route"], next(count))

            def wide(v):
                return v[:].unsqueeze(2).to_broadcast([P, NT, E])

            def by_expert(c0):
                return cst[:, c0:c0 + E].unsqueeze(1).to_broadcast([P, NT, E])

            dve.wait_ge(s["lg_sb"], NGR)
            route(dve.tensor_reduce(lmax[:], logit[:], AX.X, ALU.max))
            dve.tensor_tensor(biased[:], logit[:], wide(lmax), ALU.subtract).then_inc(s["route"], 1)
            next(count)
            dve.wait_ge(s["ex_done"], 1)
            route(dve.tensor_reduce(esum[:], ex[:], AX.X, ALU.add))
            route(dve.reciprocal(erec[:], esum[:]))
            route(dve.tensor_tensor(sc[:], ex[:], wide(erec), ALU.mult))
            route(dve.tensor_tensor(biased[:], sc[:], by_expert(C_GB), ALU.add))
            for m, ind, oh in ((m1, i1, oh1), (m2, i2, oh2)):
                route(dve.tensor_reduce(m[:], biased[:], AX.X, ALU.max))
                route(dve.tensor_tensor(eq[:], biased[:], wide(m), ALU.is_equal))
                route(dve.tensor_tensor(eq[:], eq[:], by_expert(C_IOTA), ALU.mult))
                route(dve.tensor_reduce(ind[:], eq[:], AX.X, ALU.max))
                route(dve.tensor_tensor(oh[:], by_expert(C_IOTA), wide(ind), ALU.is_equal))
                if oh is oh1:
                    route(dve.scalar_tensor_tensor(biased[:], oh1[:], NEG, biased[:], ALU.mult, ALU.add))
            route(dve.tensor_tensor(oh2[:], oh1[:], oh2[:], ALU.add))
            dve.tensor_tensor(comb[:], oh2[:], sc[:], ALU.mult).then_inc(s["comb_done"], 1)

            def add(g, e):
                r = E * g + e
                dve.wait_ge(s["y_ps"], NGR + r + 1)
                for t in range(GT):
                    xt = xall[:, bass.ds(GT * g + t, 1), :]
                    dve.scalar_tensor_tensor(xt, ps[:, 6 + e % 2, t * D:(t + 1) * D].unsqueeze(1), comb_g[:, t, e:e + 1], xt,
                                             ALU.mult, ALU.add).then_inc(s["acc_done"], 1)

            def group(g, later):
                for e in range(E):
                    r = E * g + e
                    first = not later and e == 0
                    hidden(NGR + r, e % 2, NGR if first else NGR + r - 1)
                    if e:
                        if e >= 2:
                            dve.wait_ge(s["acc_done"], GT * (r - 1))
                        else:
                            dve.wait_ge(s["comb_g_done"], g + 1)
                        add(g, e - 1)
                    elif later:
                        dve.wait_ge(s["acc_done"], GT * (r - 1))
                        add(g - 1, E - 1)
                    if e == 0:
                        if later:
                            dve.wait_ge(s["acc_done"], GT * r)
                        else:
                            dve.wait_ge(s["comb_done"], 1)
                        dve.tensor_copy(comb_g[:], comb[:, bass.ds(GT * g, GT), :]).then_inc(s["comb_g_done"], 1)

            routed_pass(dve, group)
            dve.wait_ge(s["acc_done"], GT * (E * NGR - 1))
            add(NGR - 1, E - 1)

        def moe_pool(pool):
            def step(g, new, nxt, later):
                f = g + 1
                if nxt:
                    apart(pool, "ln3_aggr", GT * f + GT)
                    pool.tensor_scalar(rstd3[:, 0, :], mv3[:, :, 1], EPS, None, ALU.add).then_inc(s["ln3_eps"], 1)
                    pool.wait_ge(s["ln3_eps"], f + 1)
                    pool.tensor_tensor(rstd3[:, 1, :], rstd3[:, 0, :], half[:], ALU.pow).then_inc(s["ln3_rstd"], 1)
                    pool.wait_ge(s["xn3T_sb"], 2 * f + 2)
                    cols = bass.ds(f * GN, GN)
                    pool.tensor_tensor(x3_lo[:, cols], xn3T, x3_hi[:].bitcast(F32)[:, cols], ALU.subtract
                                       ).then_inc(s["x3_lo_done"], 1)

            shared_pass(step)(pool)

        block = stack.enter_context(nc.Block())

        def batches(step):
            def run(eng):
                step(-1, False, False, True)
                step(0, True, False, True)
                with eng.Fori(1, B - 1) as i:
                    step(i, True, True, True)
                step(B - 1, True, True, False)
                step(B, False, True, False)
            return run

        UNITS = [(t, hf) for t in range(T) for hf in range(2)]

        @block.sync
        def _(sp):
            xt = x.rearrange("b (t p) d -> p (b t) d", p=P)
            sp.dma_start(xall[:, 0:2 * T, :], xt[:, 0:2 * T, :]).then_inc(s["x_first_in"], 16)
            sp.dma_start(cst[:], consts).then_inc(s["consts_in"], 16)
            for dst, src in ((wq_sb, wq), (wk_sb, wk), (wv_sb, wv), (wr_sb, wr), (wx_sb, wx), (gate_sb, gate)):
                sp.dma_start(dst[:], src).then_inc(s["weights_in"], 16)
            sp.dma_start(infoT[:], ctxT[0]).then_inc(s["infoT_in"], 16)
            sp.dma_start(xall[:, 2 * T:NT, :], xt[:, 2 * T:NT, :]).then_inc(s["x_in"], 16)
            sp.dma_start(w2_sb[:], w2).then_inc(s["w2_in"], 16)

            def step(i, new, old, nxt):
                if new and old:
                    apart(sp, "info_hi_done", 2 * i)
                    apart(sp, "info_lo_done", i)
                    sp.dma_start(infoT[:], ctxT[bass.ds(i, 1)].rearrange("o d m -> (o d) m")).then_inc(s["infoT_in"], 16)
                if new:
                    if old:
                        apart(sp, "w13_lo_done", i)
                    sp.dma_start(w13_raw[:], w13[bass.ds(i, 1)].rearrange("o p n -> (o p) n")).then_inc(s["w13_in"], 16)
                    apart(sp, "msplit_step", 4 * i + 4)
                    sp.dma_start(dm.rearrange("c h t -> h c t"), mparts[:]).then_inc(s["mparts_out"], 16)
                    apart(sp, "mparts_out", 16 * i + 16)
                    for a in range(HA):
                        sp.dma_start(qst[64 * a + QROWS:64 * a + KROWS].rearrange("r g t -> r (g t)"),
                                     dm[:, a * HG:(a + 1) * HG, :].rearrange("c g t -> c (g t)")
                                     ).then_inc(s["mrows_in"], 16)
                if nxt:
                    apart(sp, "split_step", 4 * i + 8)
                    for z in range(2):
                        for a in range(HA):
                            sp.dma_start(dq[z, a].rearrange("c p t -> p c t"), parts[64 * a:64 * a + 64, :, z, :]
                                         ).then_inc(s["parts_out"], 16)
                    apart(sp, "parts_out", 64 * i + 128)
                if new:
                    if old:
                        apart(sp, "xpv_ps", 4 * i)
                    sp.dma_start(info[:, 0:MB, :], ctx[bass.ds(i, 1), 0:MF, :].rearrange("o (m p) d -> p (o m) d", p=P)
                                 ).then_inc(s["info_in"], 16)
                    sp.dma_start(info[0:MR, MB, :], ctx[bass.ds(i, 1), MF:M, :].rearrange("o p d -> (o p) d")
                                 ).then_inc(s["info_in"], 16)
                if nxt:
                    rows = dq.rearrange("z a c (e g) t -> z a (c e) (g t)", e=HE)
                    for a in range(HA):
                        if new:
                            apart(sp, "gamma_ps", 12 * i + 6 * a + 6)
                        r = 64 * a
                        for n in (3, 2, 1):
                            sp.dma_start(qst[r:r + n * HE].rearrange("r g t -> r (g t)"), rows[0, a, 0:n * HE]
                                         ).then_inc(s["stack_in"], 16)
                            for m in range(n):
                                sp.dma_start(kst[r + m * HE:r + (m + 1) * HE].rearrange("r g t -> r (g t)"),
                                             rows[1, a, (3 - n) * HE:(4 - n) * HE]).then_inc(s["stack_in"], 16)
                            r += n * HE

            batches(step)(sp)
            out_tiles = out.rearrange("b (t p) d -> p (b t) d", p=P)
            with sp.Fori(0, NGR) as g:
                apart(sp, "acc_done", GT * E * g + GT * E)
                sp.dma_start(out_tiles[:, bass.ds(GT * g, GT), :], xall[:, bass.ds(GT * g, GT), :]).then_inc(s["out_done"], 16)
            sp.wait_ge(s["out_done"], 16 * NGR)

        @block.tensor
        def _(pe):
            pe.wait_ge(s["consts_in"], 16)
            pe.wait_ge(s["weights_in"], 16 * 6)
            pe.wait_ge(s["const_done"], 3)

            def step(i, new, old, nxt):
                j, f = i - 1, i + 1

                def alpha(u0, u1):
                    if not new:
                        return
                    for u in range(u0, u1):
                        n, kind = u // 3, u % 3
                        a, g0 = n // 2, 4 * (n % 2)
                        r = slice(64 * a, 64 * a + QROWS)
                        if u == 0:
                            pe.wait_ge(s["stack_in"], 16 * 18 * i + 16 * 18)
                            if old:
                                pe.wait_ge(s["p_exp"], 12 * i)
                        if u >= 2:
                            pe.wait_ge(s["alpha_max"], 12 * i + u - 1)
                        bank = ps[:, 5 + u % 2, :]
                        if kind == 0:
                            for c in range(4):
                                pe.matmul(bank[:, c * P:(c + 1) * P], lhsT=qst[r, g0 + c, 0:P], rhs=kst[r, g0 + c, 0:P],
                                          start=(c == 0), stop=False, skip_group_check=True)
                            mm = pe.matmul(bank, lhsT=ident_bf[:], rhs=mask_bf[:].rearrange("p a b -> p (a b)"),
                                           start=False, stop=True, skip_group_check=True)
                        else:
                            for c in range(2):
                                g = g0 + 2 * (kind - 1) + c
                                pe.matmul(bank[:, c * S:(c + 1) * S], lhsT=qst[r, g, P:S], rhs=kst[r, g, :],
                                          start=(c == 0), stop=False, skip_group_check=True)
                            mm = pe.matmul(bank.rearrange("p (c n) -> p c n", c=2)[:, :, P:S], lhsT=ident_bf[:],
                                           rhs=mask_bf[:, 0:2, :], start=False, stop=True, skip_group_check=True)
                        mm.then_inc(s["alpha_ps"], 1)

                def cross_scores(u):
                    t, hf = UNITS[u]
                    if u == 0:
                        pe.wait_ge(s["q2_lo_done"], j + 1)
                        pe.wait_ge(s["info_lo_done"], j + 1)
                    else:
                        pe.wait_ge(s["xexp_done"], 4 * j + u)
                    q = slice(t * P, (t + 1) * P)
                    pieces = ((0, 512), (512, H0)) if hf == 0 else ((H0, H0 + 512),)
                    for c, (m0, m1) in enumerate(pieces):
                        for n, (a, b) in enumerate(((q2_hi, info_hi), (q2_hi, info_lo), (q2_lo, info_hi))):
                            mm = pe.matmul(ps[:, c, 0:m1 - m0], lhsT=a[:, q], rhs=b[:, m0:m1], start=(n == 0), stop=(n == 2))
                    if hf == 1:
                        mm = pe.matmul(ps[:, 1, 0:TAIL], lhsT=q2[:, q], rhs=info_tail[:], start=True, stop=True)
                    mm.then_inc(s["xs_ps"], 1)

                def cross_values(u):
                    t, hf = UNITS[u]
                    blocks = range(0, 7) if hf == 0 else range(7, NB)
                    pe.wait_ge(s["xexp_done"], 4 * j + u + 1)
                    for z, part in enumerate((blocks[0:4], blocks[4:])):
                        if u >= 1:
                            pe.wait_ge(s["xt_sb"], 8 * j + 2 * u + z - 1)
                        for m in part:
                            w = P if m < MB else MR
                            o = (m - blocks[0]) * P
                            mm = pe.transpose(ps[0:w, 3 + z, (m - part[0]) * P:(m - part[0] + 1) * P], xprob[hf][:, o:o + w], ident)
                        mm.then_inc(s["xt_ps"], 1)
                    if u == 0:
                        pe.wait_ge(s["info_in"], 32 * j + 32)
                        if new:
                            pe.wait_ge(s["mT_sb"], i + 1)
                    for z, part in enumerate((blocks[0:4], blocks[4:])):
                        pe.wait_ge(s["xt_sb"], 8 * j + 2 * u + z + 1)
                        for m in part:
                            w = P if m < MB else MR
                            mm = pe.matmul(ps[:, 2, u * P:(u + 1) * P], lhsT=xprobT[hf][0:w, m - blocks[0], :], rhs=info[0:w, m, :],
                                           start=(m == blocks[0]), stop=(m == blocks[-1]))
                    mm.then_inc(s["xpv_ps"], 1)

                def gamma(n):
                    a, g0 = n // 2, 4 * (n % 2)
                    r = slice(64 * a, 64 * a + KROWS)
                    for kind in range(3):
                        v = 3 * n + kind
                        if v == 0:
                            pe.wait_ge(s["mrows_in"], 32 * i + 32)
                        if v >= 2:
                            pe.wait_ge(s["p_exp"], 12 * i + v - 1)
                        if kind < 2:
                            for c in range(2):
                                g = g0 + 2 * kind + c
                                mm = pe.matmul(ps[:, 5 + v % 2, c * S:(c + 1) * S], lhsT=kst[r, g, 0:P], rhs=qst[r, g, :],
                                               start=True, stop=True)
                        else:
                            for c in range(4):
                                mm = pe.matmul(ps[:, 5 + v % 2, c * P:(c + 1) * P], lhsT=kst[r, g0 + c, P:S],
                                               rhs=qst[r, g0 + c, P:S], start=True, stop=True)
                        mm.then_inc(s["gamma_ps"], 1)

                def values(n):
                    if n == 2 and old:
                        pe.wait_ge(s["x3_done"], 4 * j + 4)
                    if n == 2 and not old:
                        pe.wait_ge(s["mT_sb"], i + 1)
                    pe.wait_ge(s["p_masked"], 12 * i + 3 * n + 3)
                    o = ps[:, (7, 2)[n // 2], (n % 2) * S:(n % 2 + 1) * S]
                    for c in range(4):
                        pe.matmul(o[32 * c:32 * c + 32, :], lhsT=vaug[:, 0, 4 * n + c, :],
                                  rhs=prob[n % 2][:, c * S:(c + 1) * S], start=True, stop=False, skip_group_check=True)
                    for c in range(4):
                        mm = pe.matmul(o[32 * c:32 * c + 32, P:S], lhsT=vaug[:, 1, 4 * n + c, :],
                                       rhs=prob[n % 2][:, 4 * S + c * P:4 * S + (c + 1) * P], start=False, stop=True,
                                       skip_group_check=True)
                    mm.then_inc(s["pv_ps"], 1)

                if new:
                    if old:
                        pe.wait_ge(s["oT_sb"], 2 * j + 2)
                    pe.wait_ge(s["split_step"], 4 * i + 4)
                    for t in range(T):
                        mm = pe.matmul(ps[:, 7, t * P:(t + 1) * P], lhsT=xn1T[:, t * P:(t + 1) * P], rhs=wv_sb[:],
                                       start=True, stop=True)
                    mm.then_inc(s["v_ps"], 1)
                alpha(0, 1)
                if old:
                    pe.wait_ge(s["oT_sb"], 2 * j + 2)
                    for t in range(T):
                        for n in range(NG):
                            mm = pe.transpose(ps[:, 3 + t, n * P:(n + 1) * P], oT[:, n, t * P:(t + 1) * P], ident)
                    mm.then_inc(s["o_ps"], 1)
                if new:
                    pe.wait_ge(s["v_done"], i + 1)
                    v0, v1 = vaug[:, 0, :, 0:HE], vaug[:, 1, :, 0:HE]
                    pe.matmul(ps[:, 7, S:S + P], lhsT=upper, rhs=v0, start=True, stop=False)
                    pe.matmul(ps[:, 7, S:S + P], lhsT=ones, rhs=v1, start=False, stop=True)
                    pe.matmul(ps[:, 7, S + P:2 * S], lhsT=upper, rhs=v1, start=True, stop=True).then_inc(s["sv_ps"], 1)
                alpha(1, 3)
                if old:
                    pe.wait_ge(s["on_done"], j + 1)
                    for t in range(T):
                        mm = pe.transpose(ps[:, 3, t * P:(t + 1) * P], on[:, t, :], ident)
                    mm.then_inc(s["onT_ps"], 1)
                alpha(3, 4)
                if nxt:
                    pe.wait_ge(s["xn1_done"], 2 * f + 2)
                    for t in range(T):
                        mm = pe.transpose(ps[:, 2, t * P:(t + 1) * P], xn1[:, t, :], ident)
                    mm.then_inc(s["xn1T_ps"], 1)
                if old:
                    pe.wait_ge(s["onT_sb"], j + 1)
                    for t in range(T):
                        mm = pe.matmul(ps[:, 4, t * P:(t + 1) * P], lhsT=onT[:, t * P:(t + 1) * P], rhs=wr_sb[:],
                                       start=True, stop=True)
                    mm.then_inc(s["wr_ps"], 1)
                alpha(4, 6)
                if nxt:
                    pe.wait_ge(s["xn1T_sb"], f + 1)
                    if new:
                        pe.wait_ge(s["sv_sb"], i + 1)
                    pe.matmul(ps[:, 7, 0:S], lhsT=wq_sb[:], rhs=xn1T[:], start=True, stop=True)
                    pe.matmul(ps[:, 7, S:2 * S], lhsT=wk_sb[:], rhs=xn1T[:], start=True, stop=True).then_inc(s["qk_ps"], 1)
                alpha(6, 8)
                if old:
                    pe.wait_ge(s["xn2_done"], 2 * j + 2)
                    for t in range(T):
                        mm = pe.transpose(ps[:, 3, S + t * P:S + (t + 1) * P], xn2[:, t, :], ident)
                    mm.then_inc(s["xn2T_ps"], 1)
                alpha(8, 9)
                if old:
                    pe.wait_ge(s["xn2T_sb"], j + 1)
                    pe.matmul(ps[:, 4, S:2 * S], lhsT=wx_sb[:], rhs=xn2T[:], start=True, stop=True).then_inc(s["q2_ps"], 1)
                alpha(9, 10)
                if old:
                    cross_scores(0)
                alpha(10, 12)
                if new:
                    pe.wait_ge(s["negm_done"], i + 1)
                    if nxt:
                        pe.wait_ge(s["xn1T_sb"], f + 1)
                    for t in range(T):
                        mm = pe.transpose(ps[0:H, 2, S + t * P:S + (t + 1) * P], negm[:, t, :], ident)
                    mm.then_inc(s["mT_ps"], 1)
                if old:
                    for u in range(1, 4):
                        cross_scores(u)
                        cross_values(u - 1)
                if new:
                    gamma(0)
                if old:
                    cross_values(3)
                if new:
                    for n in range(NG):
                        if n + 1 < NG:
                            gamma(n + 1)
                        values(n)

            batches(step)(pe)
            moe_pe(pe)

        @block.scalar
        def _(act):
            act.wait_ge(s["consts_in"], 16)

            def step(i, new, old, nxt):
                j, f = i - 1, i + 1
                if new:
                    act.wait_ge(s["sv_ps"], i + 1)
                    act.copy(sv[:].rearrange("p t d -> p (t d)"), ps[:, 7, S:2 * S]).then_inc(s["sv_sb"], 1)
                if old:
                    act.wait_ge(s["onT_ps"], j + 1)
                    act.copy(onT[:], ps[:, 3, 0:S]).then_inc(s["onT_sb"], 1)
                if nxt:
                    act.wait_ge(s["xn1T_ps"], f + 1)
                    act.copy(xn1T[:], ps[:, 2, 0:S]).then_inc(s["xn1T_sb"], 1)
                    act.wait_ge(s["qk_ps"], f + 1)
                    for z in range(2):
                        act.activation(qk[:, z, :], ps[:, 7, z * S:(z + 1) * S], ACT.Identity,
                                       bias=cst[:, C_BIAS + z:C_BIAS + z + 1]).then_inc(s["qk_sb"], 1)
                if old:
                    act.wait_ge(s["xn2T_ps"], j + 1)
                    act.copy(xn2T[:], ps[:, 3, S:2 * S]).then_inc(s["xn2T_sb"], 1)
                    act.wait_ge(s["q2_ps"], j + 1)
                    act.activation(q2_hi[:], ps[:, 4, S:2 * S], ACT.Identity, bias=cst[:, C_BIAS + 2:C_BIAS + 3]
                                   ).then_inc(s["q2_sb"], 1)
                    act.activation(q2[:], ps[:, 4, S:2 * S], ACT.Identity, bias=cst[:, C_BIAS + 2:C_BIAS + 3]
                                   ).then_inc(s["q2_sb"], 1)

                def cross_exp(u):
                    t, hf = UNITS[u]
                    act.wait_ge(s["xmax_done"], 4 * j + u + 1)
                    if u >= 2:
                        act.wait_ge(s["xt_ps"], 8 * j + 2 * u - 2)
                    act.activation(xprob[hf][:, 0:HW[hf]], flat(0, HW[hf]), ACT.Exp, bias=xmax[:, u:u + 1],
                                   accum_out=xsum[:, u:u + 1]).then_inc(s["xexp_done"], 1)

                def cross_copy(u):
                    t, hf = UNITS[u]
                    blocks = 7 if hf == 0 else NB - 7
                    for z, (m0, m1) in enumerate(((0, 4), (4, blocks))):
                        act.wait_ge(s["xt_ps"], 8 * j + 2 * u + z + 1)
                        if u >= 2 and z == 0:
                            act.wait_ge(s["xpv_ps"], 4 * j + u - 1)
                        act.copy(xprobT[hf][:, m0:m1, :], ps[:, 3 + z, 0:(m1 - m0) * P].rearrange("p (m n) -> p m n", n=P)
                                 ).then_inc(s["xt_sb"], 1)

                if old:
                    cross_exp(0)
                if new:
                    act.wait_ge(s["negm_done"], i + 1)
                    if old:
                        act.wait_ge(s["emsv_done"], i)
                    act.activation(em[:], negm[:], ACT.Exp, scale=SCALE).then_inc(s["em_done"], 1)
                    act.wait_ge(s["mT_ps"], i + 1)
                    act.copy(mT[:], ps[0:H, 2, S:2 * S]).then_inc(s["mT_sb"], 1)
                if old:
                    for u in range(1, 4):
                        cross_copy(u - 1)
                        cross_exp(u)
                    act.wait_ge(s["xdiff_done"], j + 1)
                    act.activation(xc[:], xdiff[:], ACT.Exp).then_inc(s["xc_done"], 1)

                def p_exp(n):
                    for kind in range(3):
                        v = 3 * n + kind
                        act.wait_ge(s["gamma_ps"], 12 * i + v + 1)
                        if kind == 0 and n >= 2:
                            act.wait_ge(s["pv_ps"], NG * i + n - 1)
                        act.activation(prob[n % 2][:, kind * 512:(kind + 1) * 512], ps[:, 5 + v % 2, :], ACT.Exp, scale=SCALE
                                       ).then_inc(s["p_exp"], 1)
                if new:
                    p_exp(0)
                if old:
                    cross_copy(3)
                if new:
                    for n in range(1, NG):
                        p_exp(n)
                    act.wait_ge(s["infoT_in"], 16 * i + 16)
                    if old:
                        act.wait_ge(s["xs_ps"], 4 * i)
                    act.copy(info_hi[:], infoT[:, 0:MF3]).then_inc(s["info_hi_done"], 1)
                    act.copy(info_tail[:], infoT[:, MF3:M]).then_inc(s["info_hi_done"], 1)
                    act.wait_ge(s["w13_in"], 16 * i + 16)
                    w = w13_hi[:].rearrange("p e n -> p (e n)")
                    act.copy(w[:, bass.ds(i * WS, WS)], w13_raw[:]
                             ).then_inc(s["w13_hi_done"], 1)

            batches(step)(act)
            moe_act(act)

        @block.vector
        def _(dve):
            dve.wait_ge(s["consts_in"], 16)
            dve.tensor_copy(ident_bf[:], ident).then_inc(s["const_done"], 1)
            dve.tensor_copy(mask_bf[:], cst[:, C_MASK:C_MASK + P].unsqueeze(1).to_broadcast([P, NG, P])).then_inc(s["const_done"], 1)
            dve.memset(vaug[:], 1.0)
            dve.memset(xprob[1][:], 0.0)
            dve.memset(kst[:], 1.0).then_inc(s["const_done"], 1)
            dve.wait_ge(s["const_done"], 3)

            def step(i, new, old, nxt):
                j, f = i - 1, i + 1

                def normalised(b, mvt, r, dst, rs, done):
                    dve.wait_ge(s[rs], b + 1)
                    for t in range(T):
                        dve.tensor_scalar(dst[:, t:t + 1, :], xall[:, bass.ds(2 * b + t, 1), :], mvt[:, t, 0:1], r[:, 1, t:t + 1],
                                          ALU.subtract, ALU.mult).then_inc(s[done], 1)

                def statistics(b, stt, mvt, stats, aggr):
                    for t in range(T):
                        dve.bn_stats(stt[:, t, :], xall[:, bass.ds(2 * b + t, 1), :]).then_inc(s[stats], 1)
                    apart(dve, stats, 2 * b + 2)
                    for t in range(T):
                        dve.bn_aggr(mvt[:, t, :], stt[:, t, :]).then_inc(s[aggr], 1)

                def alpha_max(u0, u1):
                    if not new:
                        return
                    for u in range(u0, u1):
                        n, kind = u // 3, u % 3
                        dve.wait_ge(s["alpha_ps"], 12 * i + u + 1)
                        bank = ps[:, 5 + u % 2, :]
                        if kind == 0:
                            dve.tensor_reduce(mx[:, 0, 4 * n:4 * n + 4], bank.rearrange("p (c n) -> p c n", c=4), AX.X,
                                              ALU.max).then_inc(s["alpha_max"], 1)
                        else:
                            h = 4 * n + 2 * (kind - 1)
                            dve.tensor_reduce(mx[:, 1, h:h + 2], bank.rearrange("p (c n) -> p c n", c=2), AX.X,
                                              ALU.max).then_inc(s["alpha_max"], 1)

                def cross_max(u):
                    t, hf = UNITS[u]
                    dve.wait_ge(s["xs_ps"], 4 * j + u + 1)
                    dve.tensor_reduce(xmax[:, u:u + 1], flat(0, HW[hf]), AX.X, ALU.max, negate=True).then_inc(s["xmax_done"], 1)

                def three_parts(name, count, src, rest, dst):
                    dve.tensor_copy(dst[:, 0], src).then_inc(s[name], 1)
                    dve.wait_ge(s[name], 4 * count + 1)
                    dve.tensor_tensor(rest, src, dst[:, 0], ALU.subtract).then_inc(s[name], 1)
                    dve.wait_ge(s[name], 4 * count + 2)
                    dve.tensor_copy(dst[:, 1], rest).then_inc(s[name], 1)
                    dve.wait_ge(s[name], 4 * count + 3)
                    dve.tensor_tensor(dst[:, 2], rest, dst[:, 1], ALU.subtract).then_inc(s[name], 1)

                if new:
                    dve.wait_ge(s["v_ps"], i + 1)
                    dve.tensor_tensor(vaug[:, :, :, 0:HE], ps[:, 7, 0:S].rearrange("p (t h e) -> p t h e", t=T, e=HE),
                                      cst[:, C_BV:C_BV + D].rearrange("p (h e) -> p h e", e=HE).unsqueeze(1).to_broadcast([P, T, H, HE]),
                                      ALU.add).then_inc(s["v_done"], 1)
                alpha_max(0, 1)
                if nxt:
                    if not new:
                        dve.wait_ge(s["x_first_in"], 16)
                    elif old:
                        dve.wait_ge(s["x_in"], 16)
                    statistics(f, st, mv, "ln1_stats", "ln1_aggr")
                if old:
                    dve.wait_ge(s["o_ps"], j + 1)
                    dve.wait_ge(s["emc_done"], j + 1)
                    dve.wait_ge(s["emsv_done"], j + 1)
                    o = ps[:, 3:3 + T, :].rearrange("p t (h e) -> p t h e", e=32)
                    dve.tensor_tensor(den[:], o[:, :, :, HE], emc[:], ALU.add).then_inc(s["den_done"], 1)
                    dve.tensor_tensor(num[:].rearrange("p t (h e) -> p t h e", e=HE), o[:, :, :, 0:HE],
                                      emsv[:].rearrange("p t (h e) -> p t h e", e=HE), ALU.add).then_inc(s["num_done"], 1)
                    dve.wait_ge(s["den_done"], j + 1)
                    dve.reciprocal(rden[:], den[:]).then_inc(s["rden_done"], 1)
                alpha_max(1, 2)
                if nxt:
                    normalised(f, mv, rstd, xn1, "ln1_rstd", "xn1_done")
                alpha_max(2, 5)
                if old:
                    dve.wait_ge(s["wr_ps"], j + 1)
                    dve.wait_ge(s["xb_done"], j + 1)
                    dve.tensor_tensor(xall[:, bass.ds(2 * j, T), :], ps[:, 4, 0:S].rearrange("p (t d) -> p t d", t=T), xb[:],
                                      ALU.add).then_inc(s["x2_done"], 1)
                    apart(dve, "x2_done", j + 1)
                    statistics(j, st2, mv2, "ln2_stats", "ln2_aggr")
                alpha_max(5, 7)
                if old:
                    normalised(j, mv2, rstd2, xn2, "ln2_rstd", "xn2_done")
                alpha_max(7, 10)
                if old:
                    dve.wait_ge(s["q2_sb"], 2 * j + 2)
                    dve.tensor_tensor(q2_lo[:], q2[:], q2_hi[:].bitcast(F32), ALU.subtract).then_inc(s["q2_lo_done"], 1)
                alpha_max(10, 11)
                if old:
                    cross_max(0)
                alpha_max(11, 12)
                if new:
                    dve.wait_ge(s["alpha_max"], 12 * i + 12)
                    if old:
                        dve.wait_ge(s["em_done"], i)
                        dve.wait_ge(s["mT_ps"], i)
                    dve.tensor_scalar(negm[:], mx[:], 0.0, -1.0, ALU.max, ALU.mult).then_inc(s["negm_done"], 1)
                if old:
                    cross_max(1)
                if new:
                    dve.wait_ge(s["mT_sb"], i + 1)
                    if old:
                        dve.wait_ge(s["mparts_out"], 16 * i)
                    three_parts("msplit_step", i, mT[:], mT_r[:], mparts)
                if nxt:
                    dve.wait_ge(s["qk_sb"], 2 * f + 2)
                    if new:
                        dve.wait_ge(s["parts_out"], 64 * f)
                    three_parts("split_step", f, qk[:].rearrange("p z t -> p (z t)"), qk_r[:].rearrange("p z t -> p (z t)"),
                                parts[:].rearrange("p c z t -> p c (z t)"))
                if old:
                    cross_max(2)
                    cross_max(3)
                    dve.wait_ge(s["xmax_done"], 4 * j + 4)
                    n2 = xmax[:].rearrange("p (t f) -> p t f", f=2)
                    dve.tensor_tensor(xmin[:], n2[:, :, 0], n2[:, :, 1], ALU.min).then_inc(s["xmin_done"], 1)
                    dve.wait_ge(s["xden_done"], j + 1)
                    dve.reciprocal(xrec[:], xden[:]).then_inc(s["xrec_done"], 1)
                    dve.wait_ge(s["xw_done"], j + 1)
                    dve.wait_ge(s["xpv_ps"], 4 * j + 4)
                    for hf in range(2):
                        if hf:
                            dve.wait_ge(s["x3_done"], 4 * j + 2)
                        for t in range(T):
                            u = 2 * t + hf
                            dve.scalar_tensor_tensor(xall[:, bass.ds(2 * j + t, 1), :], ps[:, 2, u * P:(u + 1) * P].unsqueeze(1),
                                                     xw[:, u:u + 1], xall[:, bass.ds(2 * j + t, 1), :], ALU.mult, ALU.add
                                                     ).then_inc(s["x3_done"], 1)
                if new:
                    for n in range(2):
                        dve.wait_ge(s["pv_ps"], NG * i + 2 * n + 2)
                        dve.tensor_copy(oT[:, 2 * n:2 * n + 2, :], ps[:, (7, 2)[n], :].rearrange("p (n t) -> p n t", n=2)
                                        ).then_inc(s["oT_sb"], 1)

            batches(step)(dve)
            moe_dve(dve)

        @block.gpsimd
        def _(pool):
            pool.memset(half[:], -0.5).then_inc(s["half_done"], 1)
            pool.wait_ge(s["half_done"], 1)
            pool.wait_ge(s["consts_in"], 16)

            def inverse_deviation(b, mvt, r, aggr, eps, rs):
                apart(pool, aggr, 2 * b + 2)
                pool.tensor_scalar(r[:, 0, :], mvt[:, :, 1], EPS, None, ALU.add).then_inc(s[eps], 1)
                pool.wait_ge(s[eps], b + 1)
                pool.tensor_tensor(r[:, 1, :], r[:, 0, :], half[:, 0:T], ALU.pow).then_inc(s[rs], 1)

            def step(i, new, old, nxt):
                j, f = i - 1, i + 1
                if nxt:
                    inverse_deviation(f, mv, rstd, "ln1_aggr", "ln1_eps", "ln1_rstd")
                if old:
                    pool.wait_ge(s["rden_done"], j + 1)
                    pool.wait_ge(s["num_done"], j + 1)
                    pool.tensor_tensor(on[:].rearrange("p t (h e) -> p (t h) e", e=HE), num[:].rearrange("p t (h e) -> p (t h) e", e=HE),
                                       rden[:].rearrange("p t h -> p (t h)").unsqueeze(2).to_broadcast([P, T * H, HE]), ALU.mult
                                       ).then_inc(s["on_done"], 1)
                if old:
                    inverse_deviation(j, mv2, rstd2, "ln2_aggr", "ln2_eps", "ln2_rstd")
                if new:
                    pool.tensor_tensor(xb[:], xall[:, bass.ds(2 * i, T), :],
                                       cst[:, C_BR:C_BR + D].unsqueeze(1).to_broadcast([P, T, D]), ALU.add).then_inc(s["xb_done"], 1)
                if new:
                    pool.wait_ge(s["em_done"], i + 1)
                    pool.tensor_tensor(emc[:].rearrange("p t h -> p (t h)"), em[:].rearrange("p t h -> p (t h)"), cst[:, C_CNT:C_CNT + T * H],
                                       ALU.mult).then_inc(s["emc_done"], 1)
                    pool.wait_ge(s["sv_sb"], i + 1)
                    pool.tensor_tensor(emsv[:].rearrange("p t (h e) -> p (t h) e", e=HE), sv[:].rearrange("p t (h e) -> p (t h) e", e=HE),
                                       em[:].rearrange("p t h -> p (t h)").unsqueeze(2).to_broadcast([P, T * H, HE]), ALU.mult
                                       ).then_inc(s["emsv_done"], 1)
                if old:
                    pool.wait_ge(s["xmin_done"], j + 1)
                    n2 = xmax[:].rearrange("p (t f) -> p t f", f=2)
                    pool.tensor_tensor(xdiff[:].rearrange("p (t f) -> p t f", f=2), xmin[:].unsqueeze(2).to_broadcast([P, T, 2]), n2,
                                       ALU.subtract).then_inc(s["xdiff_done"], 1)
                    pool.wait_ge(s["xc_done"], j + 1)
                    pool.tensor_tensor(xcs[:], xc[:], xsum[:], ALU.mult).then_inc(s["xw_step"], 1)
                    pool.wait_ge(s["xw_step"], j + 1)
                    cs = xcs[:].rearrange("p (t f) -> p t f", f=2)
                    pool.tensor_tensor(xden[:], cs[:, :, 0], cs[:, :, 1], ALU.add).then_inc(s["xden_done"], 1)
                    pool.wait_ge(s["xrec_done"], j + 1)
                    pool.tensor_tensor(xw[:].rearrange("p (t f) -> p t f", f=2), xc[:].rearrange("p (t f) -> p t f", f=2),
                                       xrec[:].unsqueeze(2).to_broadcast([P, T, 2]), ALU.mult).then_inc(s["xw_done"], 1)
                if new:
                    for n in range(NG):
                        for kind in range(3):
                            apart(pool, "p_exp", 12 * i + 3 * n + kind + 1)
                            v = prob[n % 2][:, kind * 512:(kind + 1) * 512]
                            if kind < 2:
                                v = v.rearrange("p (c q) -> p c q", c=2)[:, :, 0:P]
                            else:
                                v = v.rearrange("p (c q) -> p c q", c=4)
                            pool.affine_select(out=v, in_=v, compare_op=ALU.is_gt, fill=0.0, base=0,
                                               pattern=[[0, 4 if kind == 2 else 2], [1, P]], channel_multiplier=-1
                                               ).then_inc(s["p_masked"], 1)
                    pool.wait_ge(s["info_hi_done"], 2 * i + 2)
                    pool.tensor_tensor(info_lo[:], infoT[:, 0:MF3], info_hi[:].bitcast(F32), ALU.subtract).then_inc(s["info_lo_done"], 1)
                    pool.wait_ge(s["w13_hi_done"], i + 1)
                    cols = bass.ds(i * WS, WS)
                    pool.tensor_tensor(w13_lo[:].rearrange("p e n -> p (e n)")[:, cols], w13_raw[:],
                                       w13_hi[:].rearrange("p e n -> p (e n)").bitcast(F32)[:, cols], ALU.subtract
                                       ).then_inc(s["w13_lo_done"], 1)

            batches(step)(pool)
            moe_pool(pool)


def constants(bv, br, bq, bk, bx, gate_bias):
    c = np.zeros((P, C_END), np.float32)
    q, k = np.arange(P)[:, None], np.arange(P)[None, :]
    c[:, C_ID:C_ID + P] = q == k
    c[:, C_MASK:C_MASK + P] = np.where(k >= q, np.float32(NEG), np.float32(0))
    c[:, C_U:C_U + P] = q >= k
    c[:, C_ONE:C_ONE + P] = 1
    for t in range(T):
        c[:, C_CNT + t * H:C_CNT + (t + 1) * H] = S - (t * P + q)
    c[:, C_BV:C_BV + D] = bv
    c[:, C_BR:C_BR + D] = br
    c[:, C_BIAS], c[:, C_BIAS + 1], c[:, C_BIAS + 2] = bq, bk, bx
    c[:, C_GB:C_GB + E] = gate_bias
    c[:, C_IOTA:C_IOTA + E] = E - np.arange(E)
    return c


def kernel(**inputs):
    import concourse.bacc as bacc
    from concourse.bass_utils import run_bass_kernel_spmd

    a = {n: np.asarray(v) for n, v in inputs.items()}
    wqkv, bqkv = a["L0_attn_Wqkv"], a["L0_attn_bqkv"]
    heads = np.arange(H)
    wq, wk, wv = (np.zeros((P, P), np.float32) for _ in range(3))
    for h in heads:
        rows = slice(h * HE, (h + 1) * HE)
        col = (h // HG) * 64 + np.arange(HE) * HG + h % HG
        wq[rows, col] = wqkv[:, 0:HE]
        wk[rows, col] = wqkv[:, HE:2 * HE]
        wv[rows, rows] = wqkv[:, 2 * HE:]
    order = lambda b: np.tile(np.repeat(b, HG), HA)
    consts = constants(np.tile(bqkv[2 * HE:], H), a["L0_attn_br"], order(bqkv[0:HE]), order(bqkv[HE:2 * HE]), a["L0_xattn_b"],
                       a["L0_ffn_gate_bias"])
    w1 = np.concatenate([a["L0_ffn_w1"], a["L0_ffn_sw1"][None]])
    w3 = np.concatenate([a["L0_ffn_w3"], a["L0_ffn_sw3"][None]])
    w2 = np.concatenate([a["L0_ffn_w2"], a["L0_ffn_sw2"][None]])
    arrays = {
        "x": a["x"], "ctx": a["ctx_1024"], "ctxT": a["ctx_1024"].transpose(0, 2, 1), "consts": consts,
        "wq": wq, "wk": wk, "wv": wv, "wr": a["L0_attn_Wr"], "wx": a["L0_xattn_W"].T, "gate": a["L0_ffn_gate_w"].T,
        "w13": np.concatenate([w1, w3], axis=1).reshape(B, WS, P).transpose(0, 2, 1),
        "w2": w2.reshape(NE, D, INTER // P, P).transpose(3, 0, 2, 1),
    }
    arrays = {f"in_{n}": np.ascontiguousarray(v) for n, v in arrays.items()}
    nc = bacc.Bacc("TRN2", target_bir_lowering=False, num_devices=1)
    args = [nc.dram_tensor(n, v.shape, mybir.dt.from_np(v.dtype), kind="ExternalInput").ap() for n, v in arrays.items()]
    out = nc.dram_tensor("out", (B, S, D), F32, kind="ExternalOutput").ap()
    decoder_kernel(nc, *args, out)
    r = run_bass_kernel_spmd(nc, [arrays], core_ids=[0])
    return r.results[0]["out"]
```

```python
from contextlib import ExitStack

import numpy as np
import concourse.bass as bass
from concourse import mybir

ALU = mybir.AluOpType
ACT = mybir.ActivationFunctionType
AX = mybir.AxisListType
F32 = mybir.dt.float32
F32R = mybir.dt.float32r
BF16 = mybir.dt.bfloat16

P = 128
B, S, D = 16, 256, 128
T = S // P
NT = B * T
H = 16
HE = D // H
HA = 2
HG = H // HA
NG = 4
M = 1601
MB = M // P
MR = M - MB * P
MF = MB * P
NB = MB + 1
H0 = 7 * P
MF3 = H0 + 512
TAIL = M - MF3
HW = (H0, M - H0)
E = 8
INTER = 256
GT = 4
GN = GT * P
NGR = NT // GT
NE = E + 1
WS = NE * 2 * INTER // B
EPS = 1e-5
SCALE = float(1.0 / np.sqrt(np.float32(HE)))
NEG = -1.0e30
QROWS = 48
KROWS = 51

C_ID, C_MASK, C_U, C_ONE, C_CNT, C_BV, C_BR, C_BIAS, C_GB, C_IOTA, C_END = 0, 128, 256, 384, 512, 544, 672, 800, 804, 812, 820


def decoder_kernel(nc, x, ctx, ctxT, consts, wq, wk, wv, wr, wx, gate, w13, w2, out):
    with ExitStack() as stack:
        def sb(name, shape, dt=F32):
            return stack.enter_context(nc.sbuf_tensor(name, shape, dt))

        def sem(name):
            return stack.enter_context(nc.semaphore(name))

        ps = stack.enter_context(nc.psum_tensor("banks", [P, 8, 512], F32))

        dq = nc.dram_tensor("q_parts", [HA, 3, P // HA, S], BF16).ap()
        dk = nc.dram_tensor("k_stack", [HA, 6, P // HA, S], BF16).ap()

        cst = sb("cst", [P, C_END])
        ident_bf = sb("ident_bf", [P, P], BF16)
        mask_bf = sb("mask_bf", [P, NG, P], BF16)
        minus_half = sb("minus_half", [P, 2 * T])
        wq_sb, wk_sb, wv_sb = sb("wq_sb", [P, P]), sb("wk_sb", [P, P]), sb("wv_sb", [P, P])
        wr_sb, wx_sb = sb("wr_sb", [P, P]), sb("wx_sb", [P, P])
        gate_sb = sb("gate_sb", [P, E])
        w13_raw = sb("w13_raw", [P, WS])
        w13_hi = sb("w13_hi", [P, NE, 2 * INTER], F32R)
        w13_lo = sb("w13_lo", [P, NE, 2 * INTER], F32R)
        w2_sb = sb("w2_sb", [P, NE, INTER // P, D])
        ident = cst[:, C_ID:C_ID + P]
        upper = cst[:, C_U:C_U + P]
        ones = cst[:, C_ONE:C_ONE + P]

        xall = sb("xall", [P, NT, D])

        st = sb("st", [P, T, 6])
        mv = sb("mv", [P, T, 2])
        rstd = sb("rstd", [P, 2, T])
        xn1, xn2 = sb("xn1", [P, T, D]), sb("xn2", [P, T, D])
        xb = sb("xb", [P, T, D])
        xn1T, xn2T = sb("xn1T", [P, S]), sb("xn2T", [P, S])
        st2 = sb("st2", [P, T, 6])
        mv2 = sb("mv2", [P, T, 2])
        rstd2 = sb("rstd2", [P, 2, T])

        qk = sb("qk", [P, 2, S])
        qk_r = sb("qk_r", [P, 2, S])
        parts = sb("parts", [P, 3, 2, S], BF16)
        qst, kst = sb("qst", [P, HG, S], BF16), sb("kst", [P, HG, S], BF16)
        vaug = sb("vaug", [P, T, H, 32])
        mx = sb("mx", [P, T, H])
        negm = sb("negm", [P, T, H])
        em = sb("em", [P, T, H])
        emc = sb("emc", [P, T, H])
        mT = sb("mT", [H, S])
        mT_r = sb("mT_r", [H, S])
        mparts = sb("mparts", [H, 3, S], BF16)
        sv = sb("sv", [P, T, D])
        emsv = sb("emsv", [P, T, D])
        prob = [sb(f"prob{n}", [P, 3 * 512]) for n in range(2)]
        oT = sb("oT", [P, NG, S])
        den = sb("den", [P, T, H])
        rden = sb("rden", [P, T, H])
        num = sb("num", [P, T, D])
        on = sb("on", [P, T, D])
        onT = sb("onT", [P, S])

        q2 = sb("q2", [P, S])
        q2_hi, q2_lo = sb("q2_hi", [P, S], F32R), sb("q2_lo", [P, S], F32R)
        infoT = sb("infoT", [P, M])
        info_hi, info_lo = sb("info_hi", [P, MF3], F32R), sb("info_lo", [P, MF3], F32R)
        info_tail = sb("info_tail", [P, TAIL])
        info = sb("info", [P, NB, D])
        xprob = [sb(f"xprob{n}", [P, 7 * P]) for n in range(2)]
        xprobT = [sb(f"xprobT{n}", [P, 7, P]) for n in range(2)]
        xmax, xsum, xc, xcs, xw, xdiff = (sb(n, [P, 2 * T]) for n in ("xmax", "xsum", "xc", "xcs", "xw", "xdiff"))
        xmin, xden, xrec = (sb(n, [P, T]) for n in ("xmin", "xden", "xrec"))

        s = {n: sem(n) for n in (
            "consts_in", "weights_in", "x_first_in", "x_in", "const_done", "pads_done", "w13_in",
            "ln1_stats", "ln1_aggr", "ln1_eps", "ln1_rstd", "xn1_done", "xb_done",
            "xn1T_ps", "xn1T_sb", "qk_ps", "v_ps", "qk_sb", "v_done",
            "split_cast", "split_sub", "parts0_out", "parts1_out", "stack0_in", "stack1_in",
            "sv_ps", "sv_sb", "alpha_ps", "alpha_max", "negm_done", "mT_ps", "mT_sb",
            "msplit_step", "mrows0_in", "mrows1_in", "em_done", "emc_done", "emsv_done",
            "gamma_ps", "p_exp", "p_masked", "pv_ps", "oT_sb",
            "o_ps", "den_done", "rden_done", "num_done", "on_done", "onT_ps", "onT_sb", "wr_ps", "x2_done",
            "ln2_stats", "ln2_aggr", "ln2_eps", "ln2_rstd", "xn2_done", "xn2T_ps", "xn2T_sb", "q2_ps", "q2_sb", "q2_lo_done",
            "infoT_in", "info_hi_done", "info_lo_done", "info_in",
            "xs_ps", "xmax_done", "xexp_done", "xt_ps", "xpv_ps", "xrec_done", "x3_done",
            "minus_half_done", "w2_in", "w13_hi_done", "w13_lo_done", "xt_sb", "xmin_done", "xdiff_done", "xc_done", "xw_step", "xden_done", "xw_done", "out_done")}

        def apart(eng, name, value):
            eng.wait_ge(s[name], value)
            eng.sem_inc(passed[eng.engine], 1)

        passed = {e.engine: sem(f"passed_{n}") for n, e in (("dve", nc.vector), ("pool", nc.gpsimd), ("sp", nc.sync))}

        def flat(b0, n):
            return ps[:].rearrange("p b n -> p (b n)")[:, b0 * 512:b0 * 512 + n]

        xn3, xn3T = sb("xn3", [P, GT, D]), sb("xn3T", [P, GN])
        Y_BANKS = (4, 7)
        x3_hi, x3_lo = sb("x3_hi", [P, NT * P], F32R), sb("x3_lo", [P, NT * P], F32R)
        st3, mv3, rstd3 = sb("st3", [P, GT, 6]), sb("mv3", [P, GT, 2]), sb("rstd3", [P, 2, GT])
        logit, ex, sc, biased, eq, oh1, oh2, comb = (sb(n, [P, NT, E]) for n in
                                                     ("logit", "ex", "sc", "biased", "eq", "oh1", "oh2", "comb"))
        lmax, esum, erec, m1, i1, m2, i2 = (sb(n, [P, NT]) for n in ("lmax", "esum", "erec", "m1", "i1", "m2", "i2"))
        comb_g = sb("comb_g", [P, GT, E])
        sil = [prob[z][:, 2 * GN:3 * GN] for z in range(2)]
        h = [[prob[n][:, z * GN:(z + 1) * GN] for z in range(2)] for n in range(2)]
        for n in ("ln3_stats", "ln3_aggr", "ln3_eps", "ln3_rstd", "xn3_done", "xn3T_ps", "xn3T_sb", "x3_lo_done", "lg_ps", "lg_sb",
                  "route", "ex_done", "comb_done", "comb_g_done",
                  "up_ps", "silu_done", "h_done", "y_ps", "shared_done", "acc_done"):
            s[n] = sem(n)

        def shared_step(step, g):
            step(g, g < NGR - 4, -3 <= g < NGR - 3, -2 <= g < NGR - 2, g >= 0)

        def routed_pass(eng, group):
            group(0, False)
            with eng.Fori(1, NGR) as g:
                group(g, True)

        def moe_pe(pe):
            def up(u, g, e, first=False):
                for z in range(2):
                    if not first:
                        pe.wait_ge(s["h_done"], 2 * u - 1 + z)
                    for half_w in range(2):
                        w = slice(half_w * INTER + z * P, half_w * INTER + (z + 1) * P)
                        for n, (a, b) in enumerate(((w13_hi, x3_hi), (w13_lo, x3_hi), (w13_hi, x3_lo))):
                            mm = pe.matmul(ps[:, 2 * z + half_w, :], lhsT=a[:, e, w], rhs=b[:, bass.ds(g * GN, GN)],
                                           start=(n == 0), stop=(n == 2))
                    mm.then_inc(s["up_ps"], 1)

            def down(u, e, n):
                pe.wait_ge(s["h_done"], 2 * u + 2)
                for t in range(GT):
                    for z in range(2):
                        mm = pe.matmul(ps[:, Y_BANKS[n], t * D:(t + 1) * D], lhsT=h[n][z][:, t * P:(t + 1) * P], rhs=w2_sb[:, e, z, :],
                                       start=(z == 0), stop=(z == 1))
                mm.then_inc(s["y_ps"], 1)

            def step(g, stats, norm, trans, new):
                f = g + 2
                if trans:
                    pe.wait_ge(s["xn3_done"], GT * f + GT)
                    if f:
                        pe.wait_ge(s["xn3T_sb"], 2 * f)
                    for t in range(GT):
                        mm = pe.transpose(ps[:, 5, t * P:(t + 1) * P], xn3[:, t, :], ident)
                    mm.then_inc(s["xn3T_ps"], 1)
                if new:
                    pe.wait_ge(s["x3_lo_done"], g + 1)
                    up(g, g, E, g == 0)
                if trans:
                    pe.wait_ge(s["xn3T_sb"], 2 * f + 2)
                    if f:
                        pe.wait_ge(s["lg_sb"], f)
                    for t in range(GT):
                        mm = pe.matmul(ps[:, 6, t * E:(t + 1) * E], lhsT=xn3T[:, t * P:(t + 1) * P], rhs=gate_sb[:],
                                       start=True, stop=True)
                    mm.then_inc(s["lg_ps"], 1)
                if g >= 1:
                    if g >= 3:
                        pe.wait_ge(s["shared_done"], g - 2)
                    down(g - 1, E, (g - 1) % 2)

            def rest():
                pe.wait_ge(s["w13_lo_done"], B)
                pe.wait_ge(s["w2_in"], 16)
                pe.wait_ge(s["x3_done"], 4 * B)
                pe.wait_ge(s["xt_sb"], 8 * B)
                pe.wait_ge(s["oT_sb"], 2 * B)
                pe.wait_ge(s["p_exp"], 12 * B)
                for g in range(NGR):
                    shared_step(step, g)

                def group(g, later):
                    for e in range(E):
                        r = E * g + e
                        up(NGR + r, g, e)
                        if later or e >= 3:
                            pe.wait_ge(s["acc_done"], GT * (r - 2))
                        else:
                            pe.wait_ge(s["shared_done"], NGR - 2 + e)
                        if e or later:
                            down(NGR + r - 1, (e - 1) % E, (e - 1) % 2)
                        else:
                            down(NGR - 1, E, 1)

                routed_pass(pe, group)
                pe.wait_ge(s["acc_done"], GT * (E * NGR - 2))
                down(NGR + E * NGR - 1, E - 1, 1)

            return step, rest

        def moe_act(act):
            def silu(u, first=False):
                for z in range(2):
                    act.wait_ge(s["up_ps"], 2 * u + z + 1)
                    if not first:
                        act.wait_ge(s["h_done"], 2 * u - 1 + z)
                    act.activation(sil[z], ps[:, 2 * z, :], ACT.Silu).then_inc(s["silu_done"], 1)

            def step(g, stats, norm, trans, new):
                f = g + 2
                if trans:
                    act.wait_ge(s["xn3T_ps"], f + 1)
                    if f:
                        act.wait_ge(s["lg_ps"], f)
                        act.wait_ge(s["x3_lo_done"], f)
                    act.copy(xn3T[:], ps[:, 5, :]).then_inc(s["xn3T_sb"], 1)
                    act.copy(x3_hi[:, bass.ds(f * GN, GN)], ps[:, 5, :]).then_inc(s["xn3T_sb"], 1)
                if new:
                    silu(g, g == 0)
                if g == NGR - 2:
                    act.wait_ge(s["route"], 2)
                    act.activation(ex[:], biased[:], ACT.Exp).then_inc(s["ex_done"], 1)

            def rest():
                act.wait_ge(s["pv_ps"], NG * B)
                for g in range(NGR):
                    shared_step(step, g)

                def group(g, later):
                    for e in range(E):
                        silu(NGR + E * g + e)

                routed_pass(act, group)

            return step, rest

        def moe_dve(dve):
            def hidden(u, n, read):
                if read is not None:
                    dve.wait_ge(s["y_ps"], read)
                for z in range(2):
                    dve.wait_ge(s["silu_done"], 2 * u + z + 1)
                    dve.tensor_tensor(h[n][z], ps[:, 2 * z + 1, :], sil[z], ALU.mult).then_inc(s["h_done"], 1)

            count = iter(range(1, 100))

            def route(ins):
                ins.then_inc(s["route"], 1)
                dve.wait_ge(s["route"], next(count))

            def wide(v):
                return v[:].unsqueeze(2).to_broadcast([P, NT, E])

            def by_expert(c0):
                return cst[:, c0:c0 + E].unsqueeze(1).to_broadcast([P, NT, E])

            def route_scores():
                dve.wait_ge(s["lg_sb"], NGR)
                route(dve.tensor_reduce(lmax[:], logit[:], AX.X, ALU.max))
                dve.tensor_tensor(biased[:], logit[:], wide(lmax), ALU.subtract).then_inc(s["route"], 1)
                next(count)
                dve.wait_ge(s["ex_done"], 1)
                route(dve.tensor_reduce(esum[:], ex[:], AX.X, ALU.add))
                route(dve.reciprocal(erec[:], esum[:]))
                route(dve.tensor_tensor(sc[:], ex[:], wide(erec), ALU.mult))
                route(dve.tensor_tensor(biased[:], sc[:], by_expert(C_GB), ALU.add))

            def route_best(m, ind, oh):
                route(dve.tensor_reduce(m[:], biased[:], AX.X, ALU.max))
                route(dve.tensor_tensor(eq[:], biased[:], wide(m), ALU.is_equal))
                route(dve.tensor_tensor(eq[:], eq[:], by_expert(C_IOTA), ALU.mult))
                route(dve.tensor_reduce(ind[:], eq[:], AX.X, ALU.max))
                route(dve.tensor_tensor(oh[:], by_expert(C_IOTA), wide(ind), ALU.is_equal))

            def route_first():
                route_best(m1, i1, oh1)
                route(dve.scalar_tensor_tensor(biased[:], oh1[:], NEG, biased[:], ALU.mult, ALU.add))

            def route_second():
                route_best(m2, i2, oh2)
                route(dve.tensor_tensor(oh2[:], oh1[:], oh2[:], ALU.add))
                dve.tensor_tensor(comb[:], oh2[:], sc[:], ALU.mult).then_inc(s["comb_done"], 1)

            def add_shared(g):
                dve.wait_ge(s["y_ps"], g + 1)
                xg = xall[:, bass.ds(GT * g, GT), :]
                dve.tensor_tensor(xg, ps[:, Y_BANKS[g % 2], :].rearrange("p (t d) -> p t d", t=GT), xg, ALU.add).then_inc(s["shared_done"], 1)

            def step(g, stats, norm, trans, new):
                f, m, n = g + 2, g + 3, g + 4
                if new:
                    hidden(g, g % 2, g - 1 if g >= 2 else None)
                if norm:
                    dve.wait_ge(s["ln3_rstd"], m + 1)
                    if m:
                        dve.wait_ge(s["xn3T_ps"], m)
                    for t in range(GT):
                        dve.tensor_scalar(xn3[:, t:t + 1, :], xall[:, bass.ds(GT * m + t, 1), :], mv3[:, t, 0:1], rstd3[:, 1, t:t + 1],
                                          ALU.subtract, ALU.mult).then_inc(s["xn3_done"], 1)
                if stats:
                    if n:
                        apart(dve, "xn3_done", GT * n)
                    for t in range(GT):
                        dve.bn_stats(st3[:, t, :], xall[:, bass.ds(GT * n + t, 1), :]).then_inc(s["ln3_stats"], 1)
                    apart(dve, "ln3_stats", GT * n + GT)
                    for t in range(GT):
                        dve.bn_aggr(mv3[:, t, :], st3[:, t, :]).then_inc(s["ln3_aggr"], 1)
                if trans:
                    dve.wait_ge(s["lg_ps"], f + 1)
                    dve.tensor_copy(logit[:, bass.ds(GT * f, GT), :], ps[:, 6, 0:GT * E].rearrange("p (t e) -> p t e", t=GT)
                                    ).then_inc(s["lg_sb"], 1)
                if g == NGR - 2:
                    route_scores()
                if g >= 1:
                    add_shared(g - 1)
                if g == NGR - 1:
                    route_first()

            def rest():
                apart(dve, "x3_done", 4 * B)
                for g in range(NGR):
                    shared_step(step, g)

                def add(g, e):
                    r = E * g + e
                    dve.wait_ge(s["y_ps"], NGR + r + 1)
                    for t in range(GT):
                        xt = xall[:, bass.ds(GT * g + t, 1), :]
                        dve.scalar_tensor_tensor(xt, ps[:, Y_BANKS[e % 2], t * D:(t + 1) * D].unsqueeze(1), comb_g[:, t, e:e + 1], xt,
                                                 ALU.mult, ALU.add).then_inc(s["acc_done"], 1)

                def group(g, later):
                    for e in range(E):
                        r = E * g + e
                        hidden(NGR + r, e % 2, NGR + r - 1)
                        if e:
                            if e >= 2:
                                dve.wait_ge(s["acc_done"], GT * (r - 1))
                            else:
                                dve.wait_ge(s["comb_g_done"], g + 1)
                            add(g, e - 1)
                        elif later:
                            dve.wait_ge(s["acc_done"], GT * (r - 1))
                            add(g - 1, E - 1)
                        if e == 0:
                            if later:
                                dve.wait_ge(s["acc_done"], GT * r)
                            else:
                                add_shared(NGR - 1)
                                route_second()
                                dve.wait_ge(s["comb_done"], 1)
                            dve.tensor_copy(comb_g[:], comb[:, bass.ds(GT * g, GT), :]).then_inc(s["comb_g_done"], 1)

                routed_pass(dve, group)
                dve.wait_ge(s["acc_done"], GT * (E * NGR - 1))
                add(NGR - 1, E - 1)

            return step, rest

        def moe_pool(pool):
            def step(g, stats, norm, trans, new):
                f, n = g + 2, g + 4
                if trans:
                    pool.wait_ge(s["xn3T_sb"], 2 * f + 2)
                    cols = bass.ds(f * GN, GN)
                    pool.tensor_tensor(x3_lo[:, cols], xn3T[:], x3_hi[:].bitcast(F32)[:, cols], ALU.subtract
                                       ).then_inc(s["x3_lo_done"], 1)
                if stats:
                    apart(pool, "ln3_aggr", GT * n + GT)
                    pool.tensor_scalar(rstd3[:, 0, :], mv3[:, :, 1], EPS, None, ALU.add).then_inc(s["ln3_eps"], 1)
                    pool.wait_ge(s["ln3_eps"], n + 1)
                    pool.tensor_tensor(rstd3[:, 1, :], rstd3[:, 0, :], minus_half[:], ALU.pow).then_inc(s["ln3_rstd"], 1)

            def rest():
                for g in range(NGR):
                    shared_step(step, g)


            return step, rest

        block = stack.enter_context(nc.Block())

        def batches(step):
            def run(eng):
                step(-1, True, False, False, False)
                step(0, True, True, False, False)
                step(1, True, True, True, False)
                with eng.Fori(2, B - 1) as i:
                    step(i, True, True, True, True)
                step(B - 1, False, True, True, True)
                step(B, False, False, True, True)
                step(B + 1, False, False, False, True)
            return run

        KINDS = (2, 0, 1)
        KEY_BANKS = (5, 6, 3, 4)

        UNITS = [(t, hf) for t in range(T) for hf in range(2)]

        @block.sync
        def _(sp):
            xt = x.rearrange("b (t p) d -> p (b t) d", p=P)
            sp.dma_start(xall[:, 0:2 * T, :], xt[:, 0:2 * T, :]).then_inc(s["x_first_in"], 16)
            sp.dma_start(cst[:], consts).then_inc(s["consts_in"], 16)
            for dst, src in ((wq_sb, wq), (wk_sb, wk), (wv_sb, wv), (wr_sb, wr), (wx_sb, wx), (gate_sb, gate)):
                sp.dma_start(dst[:], src).then_inc(s["weights_in"], 16)
            sp.dma_start(infoT[:], ctxT[0]).then_inc(s["infoT_in"], 16)
            sp.dma_start(xall[:, 2 * T:NT, :], xt[:, 2 * T:NT, :]).then_inc(s["x_in"], 16)
            sp.dma_start(w2_sb[:], w2).then_inc(s["w2_in"], 16)

            def write_parts(a):
                sp.dma_start(dq[a].rearrange("c p t -> p c t"), parts[64 * a:64 * a + 64, :, 0, :]).then_inc(s[f"parts{a}_out"], 16)
                for c, (s0, s1) in enumerate(((0, 3), (3, 5), (5, 6))):
                    sp.dma_start(dk[a, s0:s1].rearrange("c p t -> p c t"),
                                 parts[64 * a:64 * a + 64, c, 1, :].unsqueeze(1).to_broadcast([64, s1 - s0, S])
                                 ).then_inc(s[f"parts{a}_out"], 16)

            def step(i, nxt, new, old, crs):
                j, k, f = i - 1, i - 2, i + 1
                if old and crs:
                    apart(sp, "info_hi_done", 3 * j)
                    apart(sp, "info_lo_done", 2 * j)
                    sp.dma_start(infoT[:], ctxT[bass.ds(j, 1)].rearrange("o d m -> (o d) m")).then_inc(s["infoT_in"], 16)
                if new:
                    if old:
                        apart(sp, "w13_lo_done", i)
                    sp.dma_start(w13_raw[:], w13[bass.ds(i, 1)].rearrange("o p n -> (o p) n")).then_inc(s["w13_in"], 16)
                if nxt:
                    apart(sp, "split_sub", 2 * i + 4)
                    write_parts(0)
                if new:
                    apart(sp, "msplit_step", 4 * i + 4)
                    for a in range(HA):
                        for c in range(3):
                            sp.dma_start(qst[64 * a + QROWS + c:64 * a + QROWS + c + 1], mparts[a * HG:(a + 1) * HG, c, :]
                                         ).then_inc(s[f"mrows{a}_in"], 16)
                if nxt:
                    if not new:
                        sp.wait_ge(s["pads_done"], 2)
                    write_parts(1)
                    for a in range(HA):
                        apart(sp, f"parts{a}_out", 16 * 4 * i + 16 * 8)
                        if new:
                            apart(sp, "gamma_ps", 12 * i + 6 * a + 6)
                        r = 64 * a
                        sp.dma_start(kst[r:r + QROWS].rearrange("r g t -> r (g t)"),
                                     dk[a].rearrange("c (e g) t -> (c e) (g t)", e=HE)).then_inc(s[f"stack{a}_in"], 16)
                        for n in (3, 2, 1):
                            sp.dma_start(qst[r:r + n * HE].rearrange("r g t -> r (g t)"),
                                         dq[a, 0:n].rearrange("c (e g) t -> (c e) (g t)", e=HE)).then_inc(s[f"stack{a}_in"], 16)
                            r += n * HE
                if old:
                    if crs:
                        apart(sp, "xpv_ps", 4 * j)
                    sp.dma_start(info[:, 0:MB, :], ctx[bass.ds(j, 1), 0:MF, :].rearrange("o (m p) d -> p (o m) d", p=P)
                                 ).then_inc(s["info_in"], 16)
                    sp.dma_start(info[0:MR, MB, :], ctx[bass.ds(j, 1), MF:M, :].rearrange("o p d -> (o p) d")
                                 ).then_inc(s["info_in"], 16)

            batches(step)(sp)
            out_tiles = out.rearrange("b (t p) d -> p (b t) d", p=P)
            with sp.Fori(0, NGR) as g:
                apart(sp, "acc_done", GT * E * g + GT * E)
                sp.dma_start(out_tiles[:, bass.ds(GT * g, GT), :], xall[:, bass.ds(GT * g, GT), :]).then_inc(s["out_done"], 16)
            sp.wait_ge(s["out_done"], 16 * NGR)

        @block.tensor
        def _(pe):
            pe.wait_ge(s["consts_in"], 16)
            pe.wait_ge(s["weights_in"], 16 * 6)
            pe.wait_ge(s["const_done"], 2)

            moe_step, moe_rest = moe_pe(pe)

            def step(i, nxt, new, old, crs):
                j, k, f = i - 1, i - 2, i + 1

                def beside(g):
                    if crs and not old:
                        shared_step(moe_step, g)

                def alpha(u0, u1):
                    if not new:
                        return
                    for u in range(u0, u1):
                        n, kind = u // 3, u % 3
                        a, g0 = n // 2, 4 * (n % 2)
                        r = slice(64 * a, 64 * a + QROWS)
                        if u % 6 == 0:
                            pe.wait_ge(s[f"stack{a}_in"], 16 * 4 * i + 16 * 4)
                        if u == 0:
                            if old:
                                pe.wait_ge(s["p_exp"], 12 * i)
                        if u >= 2:
                            pe.wait_ge(s["alpha_max"], 12 * i + u - 1)
                        bank = ps[:, 5 + u % 2, :]
                        if kind == 0:
                            for c in range(4):
                                pe.matmul(bank[:, c * P:(c + 1) * P], lhsT=qst[r, g0 + c, 0:P], rhs=kst[r, g0 + c, 0:P],
                                          start=(c == 0), stop=False, skip_group_check=True)
                            mm = pe.matmul(bank, lhsT=ident_bf[:], rhs=mask_bf[:].rearrange("p a b -> p (a b)"),
                                           start=False, stop=True, skip_group_check=True)
                        else:
                            for c in range(2):
                                g = g0 + 2 * (kind - 1) + c
                                pe.matmul(bank[:, c * S:(c + 1) * S], lhsT=qst[r, g, P:S], rhs=kst[r, g, :],
                                          start=(c == 0), stop=False, skip_group_check=True)
                            mm = pe.matmul(bank.rearrange("p (c n) -> p c n", c=2)[:, :, P:S], lhsT=ident_bf[:],
                                           rhs=mask_bf[:, 0:2, :], start=False, stop=True, skip_group_check=True)
                        mm.then_inc(s["alpha_ps"], 1)

                def cross_scores(u):
                    if not crs:
                        return
                    t, hf = UNITS[u]
                    if u == 0:
                        pe.wait_ge(s["q2_lo_done"], k + 1)
                    else:
                        pe.wait_ge(s["xexp_done"], 4 * k + u)
                    if u < 2:
                        pe.wait_ge(s["info_lo_done"], 2 * k + u + 1)
                    if u == 1:
                        pe.wait_ge(s["info_hi_done"], 3 * k + 3)
                    q = slice(t * P, (t + 1) * P)
                    pieces = ((0, 512), (512, H0)) if hf == 0 else ((H0, H0 + 512),)
                    for c, (m0, m1) in enumerate(pieces):
                        for n, (a, b) in enumerate(((q2_hi, info_hi), (q2_hi, info_lo), (q2_lo, info_hi))):
                            mm = pe.matmul(ps[:, c, 0:m1 - m0], lhsT=a[:, q], rhs=b[:, m0:m1], start=(n == 0), stop=(n == 2))
                    if hf == 1:
                        mm = pe.matmul(ps[:, 1, 0:TAIL], lhsT=q2[:, q], rhs=info_tail[:], start=True, stop=True)
                    mm.then_inc(s["xs_ps"], 1)

                def halves(u):
                    blocks = range(0, 7) if UNITS[u][1] == 0 else range(7, NB)
                    return blocks, (blocks[0:4], blocks[4:])

                def cross_transposes(u):
                    if not crs:
                        return
                    hf = UNITS[u][1]
                    pe.wait_ge(s["xexp_done"], 4 * k + u + 1)
                    if u == 0 and old:
                        pe.wait_ge(s["num_done"], j + 1)
                    blocks, parts_of = halves(u)
                    for z, part in enumerate(parts_of):
                        if u >= 1:
                            pe.wait_ge(s["xt_sb"], 8 * k + 2 * u + z - 1)
                        if u == 2 and old:
                            pe.wait_ge(s[("onT_sb", "x2_done")[z]], j + 1)
                        for m in part:
                            w = P if m < MB else MR
                            o = (m - blocks[0]) * P
                            mm = pe.transpose(ps[0:w, 3 + z, (m - part[0]) * P:(m - part[0] + 1) * P], xprob[hf][:, o:o + w], ident)
                        mm.then_inc(s["xt_ps"], 1)

                def cross_values(u):
                    if not crs:
                        return
                    hf = UNITS[u][1]
                    if u == 0:
                        pe.wait_ge(s["info_in"], 32 * k + 32)
                        if new:
                            pe.wait_ge(s["sv_sb"], i + 1)
                    blocks, parts_of = halves(u)
                    for z, part in enumerate(parts_of):
                        pe.wait_ge(s["xt_sb"], 8 * k + 2 * u + z + 1)
                        for m in part:
                            w = P if m < MB else MR
                            mm = pe.matmul(ps[:, 2, u * P:(u + 1) * P], lhsT=xprobT[hf][0:w, m - blocks[0], :], rhs=info[0:w, m, :],
                                           start=(m == blocks[0]), stop=(m == blocks[-1]))
                    mm.then_inc(s["xpv_ps"], 1)

                def gamma(n):
                    if not new:
                        return
                    a, g0 = n // 2, 4 * (n % 2)
                    r = slice(64 * a, 64 * a + KROWS)
                    for z, kind in enumerate(KINDS):
                        v = 3 * n + z
                        if v % 6 == 0:
                            pe.wait_ge(s[f"mrows{a}_in"], 48 * i + 48)
                        if v >= 4:
                            pe.wait_ge(s["p_exp"], 12 * i + v - 3)
                        if kind < 2:
                            for c in range(2):
                                g = g0 + 2 * kind + c
                                mm = pe.matmul(ps[:, KEY_BANKS[v % 4], c * S:(c + 1) * S], lhsT=kst[r, g, 0:P], rhs=qst[r, g, :],
                                               start=True, stop=True)
                        else:
                            for c in range(4):
                                mm = pe.matmul(ps[:, KEY_BANKS[v % 4], c * P:(c + 1) * P], lhsT=kst[r, g0 + c, P:S],
                                               rhs=qst[r, g0 + c, P:S], start=True, stop=True)
                        mm.then_inc(s["gamma_ps"], 1)

                def values(n):
                    if not new:
                        return
                    if n == 0:
                        pe.wait_ge(s["mT_sb"], i + 1)
                    if n == 2:
                        pe.wait_ge(s["oT_sb"], 2 * i + 1)
                    pe.wait_ge(s["p_masked"], 12 * i + 3 * n + 3)
                    o = ps[:, 7, (n % 2) * S:(n % 2 + 1) * S]
                    for c in range(4):
                        pe.matmul(o[32 * c:32 * c + 32, :], lhsT=vaug[:, 0, 4 * n + c, :],
                                  rhs=prob[n % 2][:, c * S:(c + 1) * S], start=True, stop=False, skip_group_check=True)
                    for c in range(4):
                        mm = pe.matmul(o[32 * c:32 * c + 32, P:S], lhsT=vaug[:, 1, 4 * n + c, :],
                                       rhs=prob[n % 2][:, 4 * S + c * P:4 * S + (c + 1) * P], start=False, stop=True,
                                       skip_group_check=True)
                    mm.then_inc(s["pv_ps"], 1)

                alpha(0, 1)
                cross_scores(0)
                if old:
                    pe.wait_ge(s["oT_sb"], 2 * j + 2)
                    if not new:
                        pe.wait_ge(s["p_exp"], 12 * i)
                if new:
                    for t in range(T):
                        mm = pe.matmul(ps[:, 2, t * P:(t + 1) * P], lhsT=xn1T[:, t * P:(t + 1) * P], rhs=wv_sb[:],
                                       start=True, stop=True)
                    mm.then_inc(s["v_ps"], 1)
                alpha(1, 3)
                if old:
                    for t in range(T):
                        for n in range(NG):
                            mm = pe.transpose(ps[:, 3 + t, n * P:(n + 1) * P], oT[:, n, t * P:(t + 1) * P], ident)
                    mm.then_inc(s["o_ps"], 1)
                if new:
                    pe.wait_ge(s["v_done"], i + 1)
                    v0, v1 = vaug[:, 0, :, 0:HE], vaug[:, 1, :, 0:HE]
                    pe.matmul(ps[:, 2, S:S + P], lhsT=upper, rhs=v0, start=True, stop=False)
                    pe.matmul(ps[:, 2, S:S + P], lhsT=ones, rhs=v1, start=False, stop=True)
                    pe.matmul(ps[:, 2, S + P:2 * S], lhsT=upper, rhs=v1, start=True, stop=True).then_inc(s["sv_ps"], 1)
                alpha(3, 4)
                cross_transposes(0)
                alpha(4, 5)
                cross_scores(1)
                if nxt:
                    pe.wait_ge(s["xn1_done"], 2 * f + 2)
                    for t in range(T):
                        mm = pe.transpose(ps[:, 7, t * P:(t + 1) * P], xn1[:, t, :], ident)
                    mm.then_inc(s["xn1T_ps"], 1)
                alpha(5, 6)
                cross_values(0)
                alpha(6, 7)
                if nxt:
                    pe.wait_ge(s["xn1T_sb"], f + 1)
                    pe.matmul(ps[:, 7, 0:S], lhsT=wq_sb[:], rhs=xn1T[:], start=True, stop=True)
                    pe.matmul(ps[:, 7, S:2 * S], lhsT=wk_sb[:], rhs=xn1T[:], start=True, stop=True).then_inc(s["qk_ps"], 1)
                alpha(7, 8)
                cross_transposes(1)
                alpha(8, 9)
                if old:
                    pe.wait_ge(s["on_done"], j + 1)
                    if crs:
                        pe.wait_ge(s["xt_sb"], 8 * k + 3)
                    for t in range(T):
                        mm = pe.transpose(ps[:, 3, t * P:(t + 1) * P], on[:, t, :], ident)
                    mm.then_inc(s["onT_ps"], 1)
                cross_scores(2)
                alpha(9, 10)
                if old:
                    pe.wait_ge(s["onT_sb"], j + 1)
                    if crs:
                        pe.wait_ge(s["xt_sb"], 8 * k + 4)
                    for t in range(T):
                        mm = pe.matmul(ps[:, 4, t * P:(t + 1) * P], lhsT=onT[:, t * P:(t + 1) * P], rhs=wr_sb[:],
                                       start=True, stop=True)
                    mm.then_inc(s["wr_ps"], 1)
                alpha(10, 11)
                cross_values(1)
                alpha(11, 12)
                if crs and not old:
                    pe.wait_ge(s["p_exp"], 12 * B)
                beside(-2)
                cross_scores(3)
                if new:
                    pe.wait_ge(s["negm_done"], i + 1)
                    if nxt:
                        pe.wait_ge(s["qk_sb"], 2 * f + 2)
                    for t in range(T):
                        mm = pe.transpose(ps[0:H, 7, t * P:(t + 1) * P], negm[:, t, :], ident)
                    mm.then_inc(s["mT_ps"], 1)
                cross_transposes(2)
                cross_values(2)
                beside(-1)
                cross_transposes(3)
                if old:
                    pe.wait_ge(s["xn2_done"], 2 * j + 2)
                    if crs:
                        pe.wait_ge(s["xexp_done"], 4 * k + 4)
                    for t in range(T):
                        mm = pe.transpose(ps[:, 0, t * P:(t + 1) * P], xn2[:, t, :], ident)
                    mm.then_inc(s["xn2T_ps"], 1)
                cross_values(3)
                gamma(0)
                gamma(1)
                if old:
                    pe.wait_ge(s["xn2T_sb"], j + 1)
                    pe.matmul(ps[:, 1, 0:S], lhsT=wx_sb[:], rhs=xn2T[:], start=True, stop=True).then_inc(s["q2_ps"], 1)
                values(0)
                gamma(2)
                values(1)
                gamma(3)
                values(2)
                values(3)

            batches(step)(pe)
            moe_rest()

        @block.scalar
        def _(act):
            act.wait_ge(s["consts_in"], 16)
            act.copy(ident_bf[:], ident).then_inc(s["const_done"], 1)
            act.copy(mask_bf[:], cst[:, C_MASK:C_MASK + P].unsqueeze(1).to_broadcast([P, NG, P])).then_inc(s["const_done"], 1)

            moe_step, moe_rest = moe_act(act)

            def step(i, nxt, new, old, crs):
                j, k, f = i - 1, i - 2, i + 1

                def beside(g):
                    if crs and not old:
                        shared_step(moe_step, g)
                def cross_exp(u):
                    if not crs:
                        return
                    t, hf = UNITS[u]
                    act.wait_ge(s["xmax_done"], 4 * k + u + 1)
                    if u >= 2:
                        act.wait_ge(s["xt_ps"], 8 * k + 2 * u - 2)
                    act.activation(xprob[hf][:, 0:HW[hf]], flat(0, HW[hf]), ACT.Exp, bias=xmax[:, u:u + 1],
                                   accum_out=xsum[:, u:u + 1]).then_inc(s["xexp_done"], 1)

                def cross_copy(u):
                    if not crs:
                        return
                    t, hf = UNITS[u]
                    blocks = 7 if hf == 0 else NB - 7
                    for z, (m0, m1) in enumerate(((0, 4), (4, blocks))):
                        act.wait_ge(s["xt_ps"], 8 * k + 2 * u + z + 1)
                        if u >= 2 and z == 0:
                            act.wait_ge(s["xpv_ps"], 4 * k + u - 1)
                        act.copy(xprobT[hf][:, m0:m1, :], ps[:, 3 + z, 0:(m1 - m0) * P].rearrange("p (m n) -> p m n", n=P)
                                 ).then_inc(s["xt_sb"], 1)

                def split_cast(c):
                    if not nxt:
                        return
                    if c == 0:
                        if new:
                            act.wait_ge(s["parts0_out"], 16 * 4 * f)
                            act.wait_ge(s["parts1_out"], 16 * 4 * f)
                        act.wait_ge(s["qk_sb"], 2 * f + 2)
                    else:
                        act.wait_ge(s["split_sub"], 2 * f + 1)
                    act.copy(parts[:, c], (qk, qk_r)[c][:]).then_inc(s["split_cast"], 1)

                def p_exp(n):
                    if not new:
                        return
                    for z, kind in enumerate(KINDS):
                        v = 3 * n + z
                        act.wait_ge(s["gamma_ps"], 12 * i + v + 1)
                        if z == 0 and n >= 2:
                            act.wait_ge(s["pv_ps"], NG * i + n - 1)
                        act.activation(prob[n % 2][:, kind * 512:(kind + 1) * 512], ps[:, KEY_BANKS[v % 4], :], ACT.Exp, scale=SCALE
                                       ).then_inc(s["p_exp"], 1)

                cross_exp(0)
                if new:
                    act.wait_ge(s["sv_ps"], i + 1)
                    act.copy(sv[:].rearrange("p t d -> p (t d)"), ps[:, 2, S:2 * S]).then_inc(s["sv_sb"], 1)
                cross_copy(0)
                if nxt:
                    act.wait_ge(s["xn1T_ps"], f + 1)
                    act.copy(xn1T[:], ps[:, 7, 0:S]).then_inc(s["xn1T_sb"], 1)
                cross_exp(1)
                if nxt:
                    act.wait_ge(s["qk_ps"], f + 1)
                    for z in range(2):
                        act.activation(qk[:, z, :], ps[:, 7, z * S:(z + 1) * S], ACT.Identity,
                                       bias=cst[:, C_BIAS + z:C_BIAS + z + 1]).then_inc(s["qk_sb"], 1)
                cross_copy(1)
                if old:
                    act.wait_ge(s["onT_ps"], j + 1)
                    act.copy(onT[:], ps[:, 3, 0:S]).then_inc(s["onT_sb"], 1)
                split_cast(0)
                if new:
                    act.wait_ge(s["w13_in"], 16 * i + 16)
                    w = w13_hi[:].rearrange("p e n -> p (e n)")
                    act.copy(w[:, bass.ds(i * WS, WS)], w13_raw[:]).then_inc(s["w13_hi_done"], 1)
                split_cast(1)
                cross_exp(2)
                beside(-2)
                if new:
                    act.wait_ge(s["negm_done"], i + 1)
                    act.wait_ge(s["mT_ps"], i + 1)
                    act.copy(mT[:], ps[0:H, 7, 0:S]).then_inc(s["mT_sb"], 1)
                cross_copy(2)
                if old:
                    act.wait_ge(s["infoT_in"], 16 * j + 16)
                    if crs:
                        act.wait_ge(s["xs_ps"], 4 * k + 3)
                    act.copy(info_hi[:, 0:H0], infoT[:, 0:H0]).then_inc(s["info_hi_done"], 1)
                cross_exp(3)
                beside(-1)
                if new:
                    if old:
                        act.wait_ge(s["emsv_done"], i)
                    act.activation(em[:], negm[:], ACT.Exp, scale=SCALE).then_inc(s["em_done"], 1)
                cross_copy(3)
                if old:
                    act.wait_ge(s["xn2T_ps"], j + 1)
                    act.copy(xn2T[:], ps[:, 0, 0:S]).then_inc(s["xn2T_sb"], 1)
                p_exp(0)
                if crs:
                    act.wait_ge(s["xdiff_done"], k + 1)
                    act.activation(xc[:], xdiff[:], ACT.Exp).then_inc(s["xc_done"], 1)
                p_exp(1)
                if old:
                    if crs:
                        act.wait_ge(s["xs_ps"], 4 * k + 4)
                    act.copy(info_hi[:, H0:MF3], infoT[:, H0:MF3]).then_inc(s["info_hi_done"], 1)
                    act.copy(info_tail[:], infoT[:, MF3:M]).then_inc(s["info_hi_done"], 1)
                p_exp(2)
                p_exp(3)
                if old:
                    act.wait_ge(s["q2_ps"], j + 1)
                    for dst in (q2_hi, q2):
                        act.activation(dst[:], ps[:, 1, 0:S], ACT.Identity, bias=cst[:, C_BIAS + 2:C_BIAS + 3]).then_inc(s["q2_sb"], 1)

            batches(step)(act)
            moe_rest()

        @block.vector
        def _(dve):
            dve.wait_ge(s["consts_in"], 16)
            dve.wait_ge(s["pads_done"], 2)

            moe_step, moe_rest = moe_dve(dve)

            def step(i, nxt, new, old, crs):
                j, k, f = i - 1, i - 2, i + 1

                def beside(g):
                    if crs and not old:
                        shared_step(moe_step, g)

                def normalised(b, mvt, r, dst, rs, done):
                    dve.wait_ge(s[rs], b + 1)
                    for t in range(T):
                        dve.tensor_scalar(dst[:, t:t + 1, :], xall[:, bass.ds(2 * b + t, 1), :], mvt[:, t, 0:1], r[:, 1, t:t + 1],
                                          ALU.subtract, ALU.mult).then_inc(s[done], 1)

                def statistics(b, stt, mvt, stats, aggr):
                    for t in range(T):
                        dve.bn_stats(stt[:, t, :], xall[:, bass.ds(2 * b + t, 1), :]).then_inc(s[stats], 1)
                    apart(dve, stats, 2 * b + 2)
                    for t in range(T):
                        dve.bn_aggr(mvt[:, t, :], stt[:, t, :]).then_inc(s[aggr], 1)

                def alpha_max(u0, u1):
                    if not new:
                        return
                    for u in range(u0, u1):
                        n, kind = u // 3, u % 3
                        dve.wait_ge(s["alpha_ps"], 12 * i + u + 1)
                        bank = ps[:, 5 + u % 2, :]
                        if kind == 0:
                            dve.tensor_reduce(mx[:, 0, 4 * n:4 * n + 4], bank.rearrange("p (c n) -> p c n", c=4), AX.X,
                                              ALU.max).then_inc(s["alpha_max"], 1)
                        else:
                            h = 4 * n + 2 * (kind - 1)
                            dve.tensor_reduce(mx[:, 1, h:h + 2], bank.rearrange("p (c n) -> p c n", c=2), AX.X,
                                              ALU.max).then_inc(s["alpha_max"], 1)

                def cross_max(u):
                    if not crs:
                        return
                    t, hf = UNITS[u]
                    dve.wait_ge(s["xs_ps"], 4 * k + u + 1)
                    dve.tensor_reduce(xmax[:, u:u + 1], flat(0, HW[hf]), AX.X, ALU.max, negate=True).then_inc(s["xmax_done"], 1)

                def three_parts(name, count, src, rest, dst):
                    work = ((lambda: dve.tensor_copy(dst[:, 0], src)),
                            (lambda: dve.tensor_tensor(rest, src, dst[:, 0], ALU.subtract)),
                            (lambda: dve.tensor_copy(dst[:, 1], rest)),
                            (lambda: dve.tensor_tensor(dst[:, 2], rest, dst[:, 1], ALU.subtract)))
                    for o in range(4):
                        if o:
                            dve.wait_ge(s[name], 4 * count + o)
                        work[o]().then_inc(s[name], 1)

                alpha_max(0, 1)
                if nxt:
                    if not new:
                        dve.wait_ge(s["x_first_in"], 16)
                    elif old and not crs:
                        dve.wait_ge(s["x_in"], 16)
                    statistics(f, st, mv, "ln1_stats", "ln1_aggr")
                if new:
                    dve.wait_ge(s["v_ps"], i + 1)
                    dve.tensor_tensor(vaug[:, :, :, 0:HE], ps[:, 2, 0:S].rearrange("p (t h e) -> p t h e", t=T, e=HE),
                                      cst[:, C_BV:C_BV + D].rearrange("p (h e) -> p h e", e=HE).unsqueeze(1).to_broadcast([P, T, H, HE]),
                                      ALU.add).then_inc(s["v_done"], 1)
                cross_max(0)
                if crs and not old:
                    apart(dve, "x3_done", 4 * B - 4)
                beside(-4)
                alpha_max(1, 2)
                if old:
                    dve.wait_ge(s["o_ps"], j + 1)
                    dve.wait_ge(s["emc_done"], j + 1)
                    dve.wait_ge(s["emsv_done"], j + 1)
                    o = ps[:, 3:3 + T, :].rearrange("p t (h e) -> p t h e", e=32)
                    dve.tensor_tensor(den[:], o[:, :, :, HE], emc[:], ALU.add).then_inc(s["den_done"], 1)
                    dve.tensor_tensor(num[:].rearrange("p t (h e) -> p t h e", e=HE), o[:, :, :, 0:HE],
                                      emsv[:].rearrange("p t (h e) -> p t h e", e=HE), ALU.add).then_inc(s["num_done"], 1)
                    dve.wait_ge(s["den_done"], j + 1)
                    dve.reciprocal(rden[:], den[:]).then_inc(s["rden_done"], 1)
                alpha_max(2, 3)
                if nxt:
                    normalised(f, mv, rstd, xn1, "ln1_rstd", "xn1_done")
                alpha_max(3, 6)
                cross_max(1)
                beside(-3)
                alpha_max(6, 9)
                cross_max(2)
                beside(-2)
                alpha_max(9, 10)
                alpha_max(10, 11)
                if old:
                    dve.wait_ge(s["wr_ps"], j + 1)
                    dve.wait_ge(s["xb_done"], j + 1)
                    dve.tensor_tensor(xall[:, bass.ds(2 * j, T), :], ps[:, 4, 0:S].rearrange("p (t d) -> p t d", t=T), xb[:],
                                      ALU.add).then_inc(s["x2_done"], 1)
                alpha_max(11, 12)
                if new:
                    dve.wait_ge(s["alpha_max"], 12 * i + 12)
                    if old:
                        dve.wait_ge(s["em_done"], i)
                        dve.wait_ge(s["mT_ps"], i)
                    dve.tensor_scalar(negm[:], mx[:], 0.0, -1.0, ALU.max, ALU.mult).then_inc(s["negm_done"], 1)
                if old:
                    apart(dve, "x2_done", j + 1)
                    for t in range(T):
                        dve.bn_stats(st2[:, t, :], xall[:, bass.ds(2 * j + t, 1), :]).then_inc(s["ln2_stats"], 1)
                if new:
                    dve.wait_ge(s["mT_sb"], i + 1)
                    if old:
                        dve.wait_ge(s["mrows0_in"], 48 * i)
                        dve.wait_ge(s["mrows1_in"], 48 * i)
                    three_parts("msplit_step", i, mT[:], mT_r[:], mparts)
                if old:
                    apart(dve, "ln2_stats", 2 * j + 2)
                    for t in range(T):
                        dve.bn_aggr(mv2[:, t, :], st2[:, t, :]).then_inc(s["ln2_aggr"], 1)
                cross_max(3)
                if crs:
                    dve.wait_ge(s["xmax_done"], 4 * k + 4)
                    n2 = xmax[:].rearrange("p (t f) -> p t f", f=2)
                    dve.tensor_tensor(xmin[:], n2[:, :, 0], n2[:, :, 1], ALU.min).then_inc(s["xmin_done"], 1)
                beside(-1)
                if old:
                    normalised(j, mv2, rstd2, xn2, "ln2_rstd", "xn2_done")
                if crs:
                    dve.wait_ge(s["xden_done"], k + 1)
                    dve.reciprocal(xrec[:], xden[:]).then_inc(s["xrec_done"], 1)

                def heads_out(n):
                    if new:
                        dve.wait_ge(s["pv_ps"], NG * i + 2 * n + 2)
                        dve.tensor_copy(oT[:, 2 * n:2 * n + 2, :], ps[:, 7, :].rearrange("p (n t) -> p n t", n=2)
                                        ).then_inc(s["oT_sb"], 1)

                heads_out(0)
                if crs:
                    dve.wait_ge(s["xw_done"], k + 1)
                    dve.wait_ge(s["xpv_ps"], 4 * k + 4)
                    for hf in range(2):
                        if hf:
                            dve.wait_ge(s["x3_done"], 4 * k + 2)
                        for t in range(T):
                            u = 2 * t + hf
                            dve.scalar_tensor_tensor(xall[:, bass.ds(2 * k + t, 1), :], ps[:, 2, u * P:(u + 1) * P].unsqueeze(1),
                                                     xw[:, u:u + 1], xall[:, bass.ds(2 * k + t, 1), :], ALU.mult, ALU.add
                                                     ).then_inc(s["x3_done"], 1)
                if old:
                    dve.wait_ge(s["q2_sb"], 2 * j + 2)
                    dve.tensor_tensor(q2_lo[:], q2[:], q2_hi[:].bitcast(F32), ALU.subtract).then_inc(s["q2_lo_done"], 1)
                heads_out(1)

            batches(step)(dve)
            moe_rest()

        @block.gpsimd
        def _(pool):
            pool.memset(vaug[:], 1.0).then_inc(s["pads_done"], 1)
            pool.memset(kst[:], 1.0).then_inc(s["pads_done"], 1)
            pool.memset(minus_half[:], -0.5).then_inc(s["minus_half_done"], 1)
            pool.wait_ge(s["minus_half_done"], 1)
            pool.wait_ge(s["consts_in"], 16)

            def inverse_deviation(b, mvt, r, aggr, eps, rs):
                apart(pool, aggr, 2 * b + 2)
                pool.tensor_scalar(r[:, 0, :], mvt[:, :, 1], EPS, None, ALU.add).then_inc(s[eps], 1)
                pool.wait_ge(s[eps], b + 1)
                pool.tensor_tensor(r[:, 1, :], r[:, 0, :], minus_half[:, 0:T], ALU.pow).then_inc(s[rs], 1)

            moe_step, moe_rest = moe_pool(pool)

            def step(i, nxt, new, old, crs):
                j, k, f = i - 1, i - 2, i + 1

                def beside(g):
                    if crs and not old:
                        shared_step(moe_step, g)
                def info_low(part, cols):
                    if old:
                        pool.wait_ge(s["info_hi_done"], 3 * j + part + 1)
                        pool.tensor_tensor(info_lo[:, cols], infoT[:, cols], info_hi[:, cols].bitcast(F32), ALU.subtract
                                           ).then_inc(s["info_lo_done"], 1)

                def masked(n):
                    if not new:
                        return
                    for z, kind in enumerate(KINDS):
                        apart(pool, "p_exp", 12 * i + 3 * n + z + 1)
                        v = prob[n % 2][:, kind * 512:(kind + 1) * 512]
                        v = v.rearrange("p (c q) -> p c q", c=2)[:, :, 0:P] if kind < 2 else v.rearrange("p (c q) -> p c q", c=4)
                        pool.affine_select(out=v, in_=v, compare_op=ALU.is_gt, fill=0.0, base=0,
                                           pattern=[[0, 4 if kind == 2 else 2], [1, P]], channel_multiplier=-1
                                           ).then_inc(s["p_masked"], 1)

                for g in (-4, -3, -2):
                    beside(g)
                if nxt:
                    inverse_deviation(f, mv, rstd, "ln1_aggr", "ln1_eps", "ln1_rstd")
                if old:
                    pool.wait_ge(s["rden_done"], j + 1)
                    pool.wait_ge(s["num_done"], j + 1)
                    pool.tensor_tensor(on[:].rearrange("p t (h e) -> p (t h) e", e=HE), num[:].rearrange("p t (h e) -> p (t h) e", e=HE),
                                       rden[:].rearrange("p t h -> p (t h)").unsqueeze(2).to_broadcast([P, T * H, HE]), ALU.mult
                                       ).then_inc(s["on_done"], 1)
                if nxt:
                    pool.wait_ge(s["split_cast"], 2 * f + 1)
                    pool.tensor_tensor(qk_r[:], qk[:], parts[:, 0], ALU.subtract).then_inc(s["split_sub"], 1)
                    pool.wait_ge(s["split_cast"], 2 * f + 2)
                    pool.tensor_tensor(parts[:, 2], qk_r[:], parts[:, 1], ALU.subtract).then_inc(s["split_sub"], 1)
                if new:
                    pool.wait_ge(s["w13_hi_done"], i + 1)
                    cols = bass.ds(i * WS, WS)
                    pool.tensor_tensor(w13_lo[:].rearrange("p e n -> p (e n)")[:, cols], w13_raw[:],
                                       w13_hi[:].rearrange("p e n -> p (e n)").bitcast(F32)[:, cols], ALU.subtract
                                       ).then_inc(s["w13_lo_done"], 1)
                if old:
                    inverse_deviation(j, mv2, rstd2, "ln2_aggr", "ln2_eps", "ln2_rstd")
                if new:
                    pool.wait_ge(s["em_done"], i + 1)
                    pool.tensor_tensor(emc[:].rearrange("p t h -> p (t h)"), em[:].rearrange("p t h -> p (t h)"), cst[:, C_CNT:C_CNT + T * H],
                                       ALU.mult).then_inc(s["emc_done"], 1)
                    pool.wait_ge(s["sv_sb"], i + 1)
                    pool.tensor_tensor(emsv[:].rearrange("p t (h e) -> p (t h) e", e=HE), sv[:].rearrange("p t (h e) -> p (t h) e", e=HE),
                                       em[:].rearrange("p t h -> p (t h)").unsqueeze(2).to_broadcast([P, T * H, HE]), ALU.mult
                                       ).then_inc(s["emsv_done"], 1)
                if crs:
                    pool.wait_ge(s["xmin_done"], k + 1)
                    n2 = xmax[:].rearrange("p (t f) -> p t f", f=2)
                    pool.tensor_tensor(xdiff[:].rearrange("p (t f) -> p t f", f=2), xmin[:].unsqueeze(2).to_broadcast([P, T, 2]), n2,
                                       ALU.subtract).then_inc(s["xdiff_done"], 1)
                info_low(0, slice(0, H0))
                masked(0)
                if crs:
                    pool.wait_ge(s["xc_done"], k + 1)
                    pool.tensor_tensor(xcs[:], xc[:], xsum[:], ALU.mult).then_inc(s["xw_step"], 1)
                    pool.wait_ge(s["xw_step"], k + 1)
                    cs = xcs[:].rearrange("p (t f) -> p t f", f=2)
                    pool.tensor_tensor(xden[:], cs[:, :, 0], cs[:, :, 1], ALU.add).then_inc(s["xden_done"], 1)
                masked(1)
                masked(2)
                if crs:
                    pool.wait_ge(s["xrec_done"], k + 1)
                    pool.tensor_tensor(xw[:].rearrange("p (t f) -> p t f", f=2), xc[:].rearrange("p (t f) -> p t f", f=2),
                                       xrec[:].unsqueeze(2).to_broadcast([P, T, 2]), ALU.mult).then_inc(s["xw_done"], 1)
                beside(-1)
                masked(3)
                info_low(1, slice(H0, MF3))
                if new:
                    pool.tensor_tensor(xb[:], xall[:, bass.ds(2 * i, T), :],
                                       cst[:, C_BR:C_BR + D].unsqueeze(1).to_broadcast([P, T, D]), ALU.add).then_inc(s["xb_done"], 1)

            batches(step)(pool)
            moe_rest()


def constants(bv, br, bq, bk, bx, gate_bias):
    c = np.zeros((P, C_END), np.float32)
    q, k = np.arange(P)[:, None], np.arange(P)[None, :]
    c[:, C_ID:C_ID + P] = q == k
    c[:, C_MASK:C_MASK + P] = np.where(k >= q, np.float32(NEG), np.float32(0))
    c[:, C_U:C_U + P] = q >= k
    c[:, C_ONE:C_ONE + P] = 1
    for t in range(T):
        c[:, C_CNT + t * H:C_CNT + (t + 1) * H] = S - (t * P + q)
    c[:, C_BV:C_BV + D] = bv
    c[:, C_BR:C_BR + D] = br
    c[:, C_BIAS], c[:, C_BIAS + 1], c[:, C_BIAS + 2] = bq, bk, bx
    c[:, C_GB:C_GB + E] = gate_bias
    c[:, C_IOTA:C_IOTA + E] = E - np.arange(E)
    return c


def kernel(**inputs):
    import concourse.bacc as bacc
    from concourse.bass_utils import run_bass_kernel_spmd

    a = {n: np.asarray(v) for n, v in inputs.items()}
    wqkv, bqkv = a["L0_attn_Wqkv"], a["L0_attn_bqkv"]
    heads = np.arange(H)
    wq, wk, wv = (np.zeros((P, P), np.float32) for _ in range(3))
    for h in heads:
        rows = slice(h * HE, (h + 1) * HE)
        col = (h // HG) * 64 + np.arange(HE) * HG + h % HG
        wq[rows, col] = wqkv[:, 0:HE]
        wk[rows, col] = wqkv[:, HE:2 * HE]
        wv[rows, rows] = wqkv[:, 2 * HE:]
    order = lambda b: np.tile(np.repeat(b, HG), HA)
    consts = constants(np.tile(bqkv[2 * HE:], H), a["L0_attn_br"], order(bqkv[0:HE]), order(bqkv[HE:2 * HE]), a["L0_xattn_b"],
                       a["L0_ffn_gate_bias"])
    w1 = np.concatenate([a["L0_ffn_w1"], a["L0_ffn_sw1"][None]])
    w3 = np.concatenate([a["L0_ffn_w3"], a["L0_ffn_sw3"][None]])
    w2 = np.concatenate([a["L0_ffn_w2"], a["L0_ffn_sw2"][None]])
    arrays = {
        "x": a["x"], "ctx": a["ctx_1024"], "ctxT": a["ctx_1024"].transpose(0, 2, 1), "consts": consts,
        "wq": wq, "wk": wk, "wv": wv, "wr": a["L0_attn_Wr"], "wx": a["L0_xattn_W"].T, "gate": a["L0_ffn_gate_w"].T,
        "w13": np.concatenate([w1, w3], axis=1).reshape(B, WS, P).transpose(0, 2, 1),
        "w2": w2.reshape(NE, D, INTER // P, P).transpose(3, 0, 2, 1),
    }
    arrays = {f"in_{n}": np.ascontiguousarray(v) for n, v in arrays.items()}
    nc = bacc.Bacc("TRN2", target_bir_lowering=False, num_devices=1)
    args = [nc.dram_tensor(n, v.shape, mybir.dt.from_np(v.dtype), kind="ExternalInput").ap() for n, v in arrays.items()]
    out = nc.dram_tensor("out", (B, S, D), F32, kind="ExternalOutput").ap()
    decoder_kernel(nc, *args, out)
    r = run_bass_kernel_spmd(nc, [arrays], core_ids=[0])
    return r.results[0]["out"]
```
